# Optimizing a Trainium2 kernel written in Bass

```python
import numpy as np
import jax
import jax.numpy as jnp

def _softmax(x, axis=-1):
    return jax.nn.softmax(x, axis=axis)

def _gelu(x):
    return jax.nn.gelu(x, approximate=True)

def _silu(x):
    return jax.nn.silu(x)

def _sigmoid(x):
    return jax.nn.sigmoid(x)

def _layernorm(x, axis=-1, eps=1e-05):
    m = jnp.mean(x, axis=axis, keepdims=True)
    v = jnp.var(x, axis=axis, keepdims=True)
    return (x - m) / jnp.sqrt(v + eps)

def _scatter_add(tgt, idx, src, axis=0):
    return tgt.at[idx].add(src)

def _segment_sum(src, seg, n):
    return jax.ops.segment_sum(src, seg, n)
kernel_name = 'mk_xattn_ffn_d1_seqx_r4_959b85'

def setup_inputs(seed: int=0):
    np.random.seed(seed)
    _w = jnp.asarray

    def _rec_inputs():
        import jax
        import jax.numpy as jnp
        _rk = jax.random.key(seed)
        x = -0.0002928 + 1 * jax.random.normal(jax.random.fold_in(_rk, 1), (4, 512, 256), jnp.float32)
        _lenS = 512 - jax.random.randint(jax.random.fold_in(_rk, 7), (4,), 0, max(1, 512 // 4) + 1, jnp.int32)
        _lenS2 = 1024 - jax.random.randint(jax.random.fold_in(_rk, 8), (4,), 0, max(1, 1024 // 4) + 1, jnp.int32)
        _ctx_512P = jax.random.normal(jax.random.fold_in(_rk, 11), (4, 16, 128), jnp.float32)
        _ctx_512c = jax.random.dirichlet(jax.random.fold_in(_rk, 511), 0.3 * jnp.ones((16,), jnp.float32), (4, 1024))
        _ctx_512t = jnp.einsum('bsk,bkd->bsd', _ctx_512c, _ctx_512P)
        _ctx_512t = _ctx_512t * jax.lax.rsqrt(jnp.mean(jnp.square(_ctx_512t)) + 1e-12) * 0.953939
        ctx_512 = 0.00222621 + 0.99962 * (_ctx_512t + 0.3 * jax.random.normal(jax.random.fold_in(_rk, 611), (4, 1024, 128), jnp.float32))
        return (x, ctx_512)
    x, ctx_512 = _rec_inputs()

    def _L0_xattn_setup():
        import jax, jax.numpy as jnp
        import numpy as np
        B, T, TC, C, CC, H = (2, 512, 128, 256, 128, 16)
        D = C // H

        def _heads(t):
            b, l, _ = t.shape
            return t.reshape(b, l, H, D).transpose(0, 2, 1, 3)
        key = jax.random.key(seed)
        ks = jax.random.split(key, 18)
        w = lambda k, i, o: jax.random.normal(k, (i, o), jnp.float32) / np.sqrt(i).astype(np.float32)
        return {'x': jax.random.normal(ks[0], (B, T, C), jnp.float32), 'cross_input': jax.random.normal(ks[1], (B, TC, CC), jnp.float32), 'Wk': w(ks[2], C, C), 'bk': jnp.zeros((C,), jnp.float32), 'Wq': w(ks[3], C, C), 'bq': jnp.zeros((C,), jnp.float32), 'Wv': w(ks[4], C, C), 'bv': jnp.zeros((C,), jnp.float32), 'Wck': w(ks[5], CC, C), 'bck': jnp.zeros((C,), jnp.float32), 'Wcq': w(ks[6], C, C), 'bcq': jnp.zeros((C,), jnp.float32), 'Wcv': w(ks[7], CC, C), 'bcv': jnp.zeros((C,), jnp.float32), 'Wp': w(ks[8], C, C), 'bp': jnp.zeros((C,), jnp.float32)}
    _L0_xattn_all = _L0_xattn_setup()
    _L0_xattn_in = {k: v for k, v in _L0_xattn_all.items() if k in ('Wk', 'bk', 'Wq', 'bq', 'Wv', 'bv', 'Wck', 'bck', 'Wcq', 'bcq', 'Wcv', 'bcv', 'Wp', 'bp')}
    del _L0_xattn_all

    def _L0_ffn_setup():
        import jax, jax.numpy as jnp
        import numpy as np
        B, L, D = (2, 256, 256)
        HID, E, K = (512, 8, 2)
        key = jax.random.key(seed)
        ks = jax.random.split(key, 4)
        std = 0.02
        return {'x': jax.random.normal(ks[0], (B, L, D), dtype=jnp.float32), 'router_scale': jnp.ones((D,), dtype=jnp.float32), 'router_w': jax.random.normal(ks[1], (D, E), dtype=jnp.float32) * std, 'gating_w': jax.random.normal(ks[2], (E, 2, HID, D), dtype=jnp.float32) * std, 'linear_w': jax.random.normal(ks[3], (E, HID, D), dtype=jnp.float32) * std, 'per_expert_scale': jnp.ones((E,), dtype=jnp.float32)}
    _L0_ffn_all = _L0_ffn_setup()
    _L0_ffn_in = {k: v for k, v in _L0_ffn_all.items() if k in ('router_scale', 'router_w', 'gating_w', 'linear_w', 'per_expert_scale')}
    del _L0_ffn_all
    return {'x': x, 'ctx_512': ctx_512, 'L0_xattn_Wk': _L0_xattn_in['Wk'], 'L0_xattn_bk': _L0_xattn_in['bk'], 'L0_xattn_Wq': _L0_xattn_in['Wq'], 'L0_xattn_bq': _L0_xattn_in['bq'], 'L0_xattn_Wv': _L0_xattn_in['Wv'], 'L0_xattn_bv': _L0_xattn_in['bv'], 'L0_xattn_Wck': _L0_xattn_in['Wck'], 'L0_xattn_bck': _L0_xattn_in['bck'], 'L0_xattn_Wcq': _L0_xattn_in['Wcq'], 'L0_xattn_bcq': _L0_xattn_in['bcq'], 'L0_xattn_Wcv': _L0_xattn_in['Wcv'], 'L0_xattn_bcv': _L0_xattn_in['bcv'], 'L0_xattn_Wp': _L0_xattn_in['Wp'], 'L0_xattn_bp': _L0_xattn_in['bp'], 'L0_ffn_router_scale': _L0_ffn_in['router_scale'], 'L0_ffn_router_w': _L0_ffn_in['router_w'], 'L0_ffn_gating_w': _L0_ffn_in['gating_w'], 'L0_ffn_linear_w': _L0_ffn_in['linear_w'], 'L0_ffn_per_expert_scale': _L0_ffn_in['per_expert_scale']}

def reference(x, ctx_512, L0_xattn_Wk, L0_xattn_bk, L0_xattn_Wq, L0_xattn_bq, L0_xattn_Wv, L0_xattn_bv, L0_xattn_Wck, L0_xattn_bck, L0_xattn_Wcq, L0_xattn_bcq, L0_xattn_Wcv, L0_xattn_bcv, L0_xattn_Wp, L0_xattn_bp, L0_ffn_router_scale, L0_ffn_router_w, L0_ffn_gating_w, L0_ffn_linear_w, L0_ffn_per_expert_scale):
    import jax
    import jax.numpy as jnp

    def _L0_xattn_ref(x, cross_input, Wk, bk, Wq, bq, Wv, bv, Wck, bck, Wcq, bcq, Wcv, bcv, Wp, bp):
        import jax, jax.numpy as jnp
        import numpy as np
        B, T, TC, C, CC, H = (2, 512, 128, 256, 128, 16)
        D = C // H

        def _heads(t):
            b, l, _ = t.shape
            return t.reshape(b, l, H, D).transpose(0, 2, 1, 3)
        scale = np.float32(1.0 / np.sqrt(D))
        q = _heads(x @ Wq + bq)
        k = _heads(x @ Wk + bk)
        v = _heads(x @ Wv + bv)
        att = jnp.einsum('bhqd,bhkd->bhqk', q, k) * scale
        causal = jnp.tril(jnp.ones((T, T), bool))
        att = jnp.where(causal[None, None], att, -jnp.inf)
        y = jnp.einsum('bhqk,bhkd->bhqd', jax.nn.softmax(att, axis=-1), v)
        qc = _heads(x @ Wcq + bcq)
        kc = _heads(cross_input @ Wck + bck)
        vc = _heads(cross_input @ Wcv + bcv)
        attc = jnp.einsum('bhqd,bhkd->bhqk', qc, kc) * scale
        y = y + jnp.einsum('bhqk,bhkd->bhqd', jax.nn.softmax(attc, axis=-1), vc)
        y = y.transpose(0, 2, 1, 3).reshape(x.shape[0], T, C)
        return y @ Wp + bp

    def _L0_ffn_ref(x, router_scale, router_w, gating_w, linear_w, per_expert_scale):
        import jax, jax.numpy as jnp
        import numpy as np
        B, L, D = (2, 256, 256)
        HID, E, K = (512, 8, 2)
        d = x.shape[-1]
        var = jnp.mean(jnp.square(x), axis=-1, keepdims=True)
        r_in = x * jax.lax.rsqrt(var + 1e-06)
        r_in = r_in * jax.lax.rsqrt(jnp.array(d, dtype=r_in.dtype)) * router_scale
        logits = jnp.dot(r_in, router_w).astype(jnp.float32)
        probs = jax.nn.softmax(logits, axis=-1)
        _, top_k_idx = jax.lax.top_k(logits, K)
        indicator = jax.nn.one_hot(top_k_idx, probs.shape[-1], dtype=probs.dtype)
        gate_weights = indicator.sum(axis=-2) * probs
        renorm = jnp.sum(gate_weights, axis=-1, keepdims=True)
        renorm = jnp.where(renorm > 0.0, renorm, 1.0)
        weights = probs / renorm
        top_k_w = jnp.take_along_axis(weights, top_k_idx, axis=-1)
        combine = jnp.einsum('blke,blk->ble', indicator, top_k_w)
        combine = combine * per_expert_scale
        gate0 = jnp.einsum('bld,ehd->bleh', x, gating_w[:, 0])
        gate1 = jnp.einsum('bld,ehd->bleh', x, gating_w[:, 1])
        act = jax.nn.gelu(gate0) * gate1
        out = jnp.einsum('bleh,ehd,ble->bld', act, linear_w, combine)
        return out.astype(x.dtype)
    x = x + _L0_xattn_ref(_layernorm(x, axis=-1), ctx_512, L0_xattn_Wk, L0_xattn_bk, L0_xattn_Wq, L0_xattn_bq, L0_xattn_Wv, L0_xattn_bv, L0_xattn_Wck, L0_xattn_bck, L0_xattn_Wcq, L0_xattn_bcq, L0_xattn_Wcv, L0_xattn_bcv, L0_xattn_Wp, L0_xattn_bp)
    x = x + _L0_ffn_ref(_layernorm(x, axis=-1), L0_ffn_router_scale, L0_ffn_router_w, L0_ffn_gating_w, L0_ffn_linear_w, L0_ffn_per_expert_scale)
    return x

_drawn_inputs = setup_inputs


def setup_inputs(seed=0):
    import zlib

    import numpy as np

    out = dict(_drawn_inputs(seed))
    spreads = {'L0_xattn_bk': (0.0, 0.8),
     'L0_xattn_bq': (0.0, 0.615),
     'L0_xattn_bv': (0.0, 0.1),
     'L0_xattn_bck': (0.0, 0.8),
     'L0_xattn_bcq': (0.0, 0.423),
     'L0_xattn_bcv': (0.0, 0.1),
     'L0_xattn_bp': (0.0, 0.1),
     'L0_ffn_router_scale': (1.0, 0.6),
     'L0_ffn_per_expert_scale': (1.0, 0.6)}
    factors = {'L0_ffn_router_w': 4.186, 'L0_ffn_gating_w': 3.662, 'L0_ffn_linear_w': 3.636}
    for name, (base, spread) in spreads.items():
        noise = np.random.default_rng([zlib.crc32(name.encode()), seed]).standard_normal(out[name].shape)
        drawn = base * np.exp(spread * noise) if base else spread * noise
        out[name] = jnp.asarray(drawn.astype(out[name].dtype))
    for name, factor in factors.items():
        out[name] = (out[name] * factor).astype(out[name].dtype)
    return out
```

```python
from contextlib import ExitStack

import numpy as np
import concourse.bass as bass
from concourse import mybir

F32 = mybir.dt.float32
BF16 = mybir.dt.bfloat16
I32 = mybir.dt.int32
ACT = mybir.ActivationFunctionType
ALU = mybir.AluOpType
AX = mybir.AxisListType

P = 128
B, T, C = 4, 512, 256
TC, CC = 1024, 128
H = 16
D = C // H
CH = C // P
QT = T // P
KS, KC = T // P, TC // P
GH = 4
NG = B * H // GH
VW = 32
E = 8
NSPLIT = 3
PAIR_ROWS = 6 * D
SHIFT_ROWS = NSPLIT
MASKED = -1.0e38
SCALE = float(D) ** -0.5
LN_EPS = 1e-5
RMS_EPS = 1e-6


def reached(eng, sem, count):
    if not (isinstance(count, int) and count <= 0):
        eng.wait_ge(sem, count)


ROOT_STEPS = 6


def inverse_root(dve, var, eps, root, out, step, done, root_ready, roots, scale=1.0):
    dve.wait_ge(step, done)
    dve.tensor_scalar(root[:, 0, :], var, scale, eps, ALU.mult, ALU.add).then_inc(step, 1)
    dve.wait_ge(root_ready, roots)
    dve.reciprocal(out, root[:, 1, :]).then_inc(step, 1)
    dve.wait_ge(step, done + 2)
    dve.tensor_tensor(root[:, 2, :], out, out, ALU.mult).then_inc(step, 1)
    dve.wait_ge(step, done + 3)
    dve.tensor_tensor(root[:, 2, :], root[:, 2, :], root[:, 0, :], ALU.mult).then_inc(step, 1)
    dve.wait_ge(step, done + 4)
    dve.tensor_scalar(root[:, 2, :], root[:, 2, :], -0.5, 1.5, ALU.mult, ALU.add).then_inc(step, 1)
    dve.wait_ge(step, done + 5)
    dve.tensor_tensor(out, out, root[:, 2, :], ALU.mult).then_inc(step, 1)
    dve.wait_ge(step, done + 6)


def reached_apart(eng, sem, count, passed):
    if not (isinstance(count, int) and count <= 0):
        eng.wait_ge(sem, count)
        eng.sem_inc(passed, 1)


CTX_JOBS = [("split", "kc", 0, 0), ("value", KS + 0), ("value", KS + 1),
            ("split", "kc", 1, 0), ("value", KS + 2), ("value", KS + 3),
            ("split", "kc", 0, 1), ("value", KS + 4), ("value", KS + 5),
            ("split", "kc", 1, 1), ("value", KS + 6), ("value", KS + 7)]
SELF_JOBS = [("split", "q", 0, 0), ("value", 0), ("split", "q", 1, 0), ("value", 1),
             ("split", "k", 0, 0), ("value", 2), ("split", "k", 1, 0), ("value", 3),
             ("split", "qc", 0, 0), ("split", "qc", 1, 0)]
JOBS = CTX_JOBS + SELF_JOBS
NS = sum(j[0] == "split" for j in JOBS)
NV = len(JOBS) - NS
LN_STEPS = 2 * QT + ROOT_STEPS
S_PSUM, V_PSUM, PARTS, V_SB = 5, 2, 5, 4
assert NS % S_PSUM == 0 and NS % PARTS == 0 and NV % V_SB == 0 and NS % 2 == 0 and NV % V_PSUM == 0


def build_projections(nc, a, scr):
    with ExitStack() as ctx:
        def sb(name, shape, dt=F32):
            return ctx.enter_context(nc.sbuf_tensor(name, shape, dt))

        def sem(name):
            return ctx.enter_context(nc.semaphore(name))

        x_in = sb("x_in", [P, QT, C])
        ctx_in = sb("ctx_in", [P, TC])
        w_in = {n: sb(f"w_{n}", [P, CH, C]) for n in ("q", "k", "v", "qc")}
        wc_in = {n: sb(f"w_{n}", [P, C]) for n in ("kc", "vc")}
        b_col = {n: sb(f"b_{n}", [P, CH]) for n in ("q", "k", "qc", "kc")}
        b_row = {n: sb(f"b_{n}", [P, C]) for n in ("v", "vc")}
        ident = sb("ident_a", [P, P])
        stats = sb("stats_a", [P, QT, 6])
        mean_var = sb("mean_var_a", [P, QT, 2])
        rstd = sb("rstd_a", [P, QT])
        root = sb("root_a", [P, 3, QT])
        xn = sb("xn", [P, QT, C])
        xnT = sb("xnT", [P, CH, T])
        proj = sb("proj", [P, 2, T])
        rest = sb("rest", [P, 2, T])
        parts = sb("parts", [P, PARTS, NSPLIT, T], BF16)
        v_out = sb("v_out", [P, V_SB, H, VW])
        ps_split = [ctx.enter_context(nc.psum_tensor(f"ps_split{i}", [P, T], F32)) for i in range(S_PSUM)]
        ps_value = [ctx.enter_context(nc.psum_tensor(f"ps_value{i}", [P, T], F32)) for i in range(V_PSUM)]
        ps_xT = ctx.enter_context(nc.psum_tensor("ps_xT", [P, T], F32))

        w_loaded, b_loaded, x_loaded, ctx_loaded = sem("w_loaded"), sem("b_loaded"), sem("x_loaded"), sem("ctx_loaded")
        ident_ready, v_ready = sem("ident_a_ready"), sem("v_pads_ready")
        ln_step, root_ready, xn_ready = sem("ln_step_a"), sem("root_a_ready"), sem("xn_ready")
        xT_ready, xT_copied = sem("xT_ready"), sem("xT_copied")
        split_mm, part1 = sem("split_mm"), sem("part1")
        rest1, part2, part3 = sem("rest1"), sem("part2"), sem("part3")
        part_stored = [sem(f"part_stored{i}") for i in range(PARTS)]
        value_mm, value_copied = sem("value_mm"), sem("value_copied")
        value_stored = [sem(f"value_stored{i}") for i in range(V_SB)]
        N_MATRICES, N_BIASES = 6, 6

        dve_passed, pool_passed, sp_passed = sem("dve_passed_a"), sem("pool_passed_a"), sem("sp_passed_a")
        block = ctx.enter_context(nc.Block())

        @block.sync
        def _(sp):
            def load_ctx(b):
                sp.dma_start(ctx_in[:, :], a["ctxT"][b]).then_inc(ctx_loaded, 16)

            def load_x(b):
                sp.dma_start(x_in[:, :, :], a["x"][b].rearrange("(j p) c -> p j c", p=P)).then_inc(x_loaded, 16)

            load_ctx(0)
            for n, src in (("kc", "Wck"), ("vc", "Wcv")):
                sp.dma_start(wc_in[n][:, :], a[src]).then_inc(w_loaded, 16)
            load_x(0)
            for n, src in (("q", "Wq"), ("k", "Wk"), ("v", "Wv"), ("qc", "Wcq")):
                sp.dma_start(w_in[n][:, :, :], a[src].rearrange("(c p) n -> p c n", p=P)).then_inc(w_loaded, 16)

            def body(b, last):
                s = v = 0
                for job in JOBS:
                    if job[0] == "split":
                        _, dst, m, blk = job
                        reached_apart(sp, part3, b * NS + s + 1 + 2, sp_passed)
                        cols = slice(blk * T, (blk + 1) * T)
                        for p in range(NSPLIT):
                            sp.dma_start(scr[dst][b, m * (P // D):(m + 1) * (P // D), p, :, cols],
                                         parts[:, s % PARTS, p, :]).then_inc(part_stored[s % PARTS], 16)
                        s += 1
                    else:
                        reached_apart(sp, value_copied, b * NV + v + 1 + V_PSUM, sp_passed)
                        sp.dma_start(scr["v"][b, :, :, job[1], :].rearrange("g p f -> p g f"),
                                     v_out[:, v % V_SB].rearrange("p (g j) f -> p g (j f)", j=GH))\
                          .then_inc(value_stored[v % V_SB], 16)
                        v += 1
                    if job == CTX_JOBS[-1] and not last:
                        sp.wait_ge(xn_ready, b + 1)
                        load_x(b + 1)
                        sp.wait_ge(value_mm, b * NV + KC)
                        load_ctx(b + 1)

            with sp.Fori(0, B - 1) as b:
                body(b, False)
            body(B - 1, True)
            for i in range(PARTS):
                sp.wait_ge(part_stored[i], 16 * (B * (NS // PARTS) + 1) * NSPLIT)
            for i in range(V_SB):
                sp.wait_ge(value_stored[i], 16 * (B * (NV // V_SB) + 1))

        @block.gpsimd
        def _(pool):
            for q in part_stored:
                pool.sem_inc(q, 16 * NSPLIT)
            for n, src in (("q", "bq"), ("k", "bk"), ("qc", "bcq"), ("kc", "bck")):
                pool.dma_start(b_col[n][:, :], a[src]).then_inc(b_loaded, 16)
            for n, src in (("v", "bv"), ("vc", "bcv")):
                pool.dma_start(b_row[n][:, :], a[src].rearrange("(o n) -> o n", o=1).to_broadcast([P, C]))\
                    .then_inc(b_loaded, 16)
            pool.memset(ident[:, :], 0.0).then_inc(ident_ready, 1)
            pool.wait_ge(ident_ready, 1)
            pool.affine_select(out=ident[:, :], in_=ident[:, :], compare_op=ALU.not_equal, fill=1.0,
                               base=0, pattern=[[-1, P]], channel_multiplier=1).then_inc(ident_ready, 1)
            with pool.Fori(0, B) as b:
                for s in range(NS):
                    reached_apart(pool, rest1, b * NS + s + 1 + 2, pool_passed)
                    pool.tensor_copy(parts[:, s % PARTS, 1, :], rest[:, s % 2, :]).then_inc(part2, 1)

        @block.scalar
        def _(act):
            act.sem_inc(part1, S_PSUM)
            act.sem_inc(xT_copied, 1)
            act.wait_ge(b_loaded, 16 * N_BIASES)
            with act.Fori(0, B) as b:
                act.wait_ge(ln_step, b * LN_STEPS + 2 * QT + 1)
                act.activation(root[:, 1, :], root[:, 0, :], ACT.Sqrt).then_inc(root_ready, 1)
                s = 0
                for job in JOBS:
                    if job == SELF_JOBS[0]:
                        for c in range(CH):
                            act.wait_ge(xT_ready, b * CH + c + 1 + CH)
                            act.activation(xnT[:, c, :], ps_xT[:, :], ACT.Identity).then_inc(xT_copied, 1)
                    if job[0] != "split":
                        continue
                    bias = b_col[job[1]][:, job[2]:job[2] + 1]
                    act.wait_ge(split_mm, b * NS + s + 1)
                    act.wait_ge(rest1, b * NS + s + 1)
                    act.activation(proj[:, s % 2, :], ps_split[s % S_PSUM][:, :], ACT.Identity, bias=bias)
                    act.wait_ge(part_stored[s % PARTS], (b * (NS // PARTS) + s // PARTS + 1) * 16 * NSPLIT)
                    act.activation(parts[:, s % PARTS, 0, :], ps_split[s % S_PSUM][:, :], ACT.Identity, bias=bias)\
                       .then_inc(part1, 1)
                    s += 1

        @block.vector
        def _(dve):
            dve.sem_inc(rest1, 2)
            dve.sem_inc(part3, 2)
            dve.sem_inc(value_copied, V_PSUM)
            for q in value_stored:
                dve.sem_inc(q, 16)
            dve.memset(v_out[:, :, :, :], 0.0).then_inc(v_ready, 1)
            dve.wait_ge(v_ready, 1)
            dve.memset(v_out[:, :, :, 0:1], 1.0).then_inc(v_ready, 1)
            dve.wait_ge(v_ready, 2)
            dve.wait_ge(b_loaded, 16 * N_BIASES)
            with dve.Fori(0, B) as b:
                dve.wait_ge(x_loaded, (b + 1) * 16)
                for j in range(QT):
                    dve.bn_stats(stats[:, j, :], x_in[:, j, :]).then_inc(ln_step, 1)
                for j in range(QT):
                    reached_apart(dve, ln_step, b * LN_STEPS + j + 1, dve_passed)
                    dve.bn_aggr(mean_var[:, j, :], stats[:, j, :]).then_inc(ln_step, 1)
                inverse_root(dve, mean_var[:, :, 1], LN_EPS, root, rstd[:, :], ln_step, b * LN_STEPS + 2 * QT,
                             root_ready, b + 1)
                dve.wait_ge(xT_ready, b * CH + CH)
                for j in range(QT):
                    ins = dve.tensor_scalar(xn[:, j, :], x_in[:, j, :], mean_var[:, j, 0:1], rstd[:, j:j + 1],
                                            ALU.subtract, ALU.mult)
                ins.then_inc(xn_ready, 1)

                def third_part(s):
                    dve.wait_ge(part2, b * NS + s + 1)
                    dve.tensor_tensor(parts[:, s % PARTS, 2, :], rest[:, s % 2, :], parts[:, s % PARTS, 1, :],
                                      ALU.subtract).then_inc(part3, 1)

                s = v = 0
                for job in JOBS:
                    if job[0] == "split":
                        dve.wait_ge(part1, b * NS + s + 1 + S_PSUM)
                        dve.wait_ge(part3, b * NS + s + 1)
                        dve.tensor_tensor(rest[:, s % 2, :], proj[:, s % 2, :], parts[:, s % PARTS, 0, :],
                                          ALU.subtract).then_inc(rest1, 1)
                        if s:
                            third_part(s - 1)
                        s += 1
                    else:
                        dve.wait_ge(value_mm, b * NV + v + 1)
                        dve.wait_ge(value_stored[v % V_SB], (b * (NV // V_SB) + v // V_SB + 1) * 16)
                        bias = b_row["v" if job[1] < KS else "vc"]
                        dve.tensor_tensor(v_out[:, v % V_SB, :, 1:1 + D],
                                          ps_value[v % V_PSUM][:, 0:C].rearrange("p (h d) -> p h d", h=H),
                                          bias[:, :].rearrange("p (h d) -> p h d", h=H), ALU.add)\
                           .then_inc(value_copied, 1)
                        v += 1
                third_part(NS - 1)

        @block.tensor
        def _(pe):
            pe.sem_inc(xT_ready, CH)
            pe.wait_ge(w_loaded, 16 * N_MATRICES)
            pe.wait_ge(ident_ready, 2)
            with pe.Fori(0, B) as b:
                pe.wait_ge(ctx_loaded, (b + 1) * 16)
                s = v = 0
                for job in JOBS:
                    if job == SELF_JOBS[0]:
                        pe.wait_ge(xn_ready, b + 1)
                        for c in range(CH):
                            pe.wait_ge(xT_copied, b * CH + c + 1)
                            for j in range(QT):
                                ins = pe.transpose(ps_xT[:, j * P:(j + 1) * P], xn[:, j, c * P:(c + 1) * P],
                                                   ident[:, :])
                            ins.then_inc(xT_ready, 1)
                        pe.wait_ge(xT_copied, b * CH + CH + 1)
                    if job[0] == "split":
                        _, name, m, blk = job
                        pe.wait_ge(part1, b * NS + s + 1)
                        out = ps_split[s % S_PSUM][:, :]
                        if name == "kc":
                            ins = pe.matmul(out, wc_in["kc"][:, m * P:(m + 1) * P], ctx_in[:, blk * T:(blk + 1) * T],
                                            start=True, stop=True)
                        else:
                            for c in range(CH):
                                ins = pe.matmul(out, w_in[name][:, c, m * P:(m + 1) * P], xnT[:, c, :],
                                                start=(c == 0), stop=(c == CH - 1))
                        ins.then_inc(split_mm, 1)
                        s += 1
                    else:
                        j = job[1]
                        pe.wait_ge(value_copied, b * NV + v + 1)
                        out = ps_value[v % V_PSUM][:, 0:C]
                        if j >= KS:
                            ins = pe.matmul(out, ctx_in[:, (j - KS) * P:(j - KS + 1) * P], wc_in["vc"][:, :],
                                            start=True, stop=True)
                        else:
                            for c in range(CH):
                                ins = pe.matmul(out, xnT[:, c, j * P:(j + 1) * P], w_in["v"][:, c, :],
                                                start=(c == 0), stop=(c == CH - 1))
                        ins.then_inc(value_mm, 1)
                        v += 1


STEPS = KS + KC
UNITS = 2 * GH * QT
SELF_UNITS = GH * QT
MAX_BANKS = 4
assert E == (NG - 2) // 2 + 1
PAIR_OF_ONES = float(np.uint32(0x3F803F80).view(np.float32))
ROWS = NSPLIT * GH * QT
LOAD_A = 16 * 9
LOAD_B = 16 * 10
Q_STACK = [(0, 3), (0, 2), (0, 1)]
K_STACK = [0, 0, 0, 1, 1, 2]


def units_of_step(k):
    if k < KS:
        return range(GH * k, GH * k + GH)
    return range(SELF_UNITS + 2 * (k - KS), SELF_UNITS + 2 * (k - KS) + 2)


def build_attention(nc, scr, y_all, experts):
    with ExitStack() as ctx:
        def sb(name, shape, dt=F32):
            return ctx.enter_context(nc.sbuf_tensor(name, shape, dt))

        def sem(name):
            return ctx.enter_context(nc.semaphore(name))

        q_self = [sb(f"q_self{i}", [P, GH, T], BF16) for i in range(2)]
        k_self = [sb(f"k_self{i}", [P, GH, T], BF16) for i in range(2)]
        q_cross = [sb(f"q_cross{i}", [P, GH, T], BF16) for i in range(2)]
        k_cross = [sb(f"k_cross{i}", [P, GH, TC], BF16) for i in range(2)]
        values = [sb(f"values{i}", [P, STEPS, GH * VW]) for i in range(2)]
        ident = sb("ident_b", [P, P])
        ident_h = sb("ident_bh", [P, P], BF16)
        mask_q = sb("mask_q", [P, P], BF16)
        mask_k = sb("mask_k", [P, P], BF16)
        neg_max = [sb(f"neg_max{i}", [P, GH * QT]) for i in range(2)]
        neg_rest = [sb(f"neg_rest{i}", [P, GH * QT]) for i in range(2)]
        neg_parts = [sb(f"neg_parts{i}", [P, NSPLIT, GH * QT], BF16) for i in range(2)]
        shift_rows = [sb(f"shift_rows{i}", [ROWS, P], BF16) for i in range(2)]
        probs = [sb(f"probs{i}", [P, GH, T]) for i in range(2)]
        sums = [sb(f"sums{i}", [P, T]) for i in range(2)]
        inv = [sb(f"inv{i}", [P, GH * QT]) for i in range(2)]
        y_cross = sb("y_cross", [P, QT, GH, D])
        ps_max = [ctx.enter_context(nc.psum_tensor(f"ps_max{i}", [P, TC], F32)) for i in range(2)]
        ps_score = [ctx.enter_context(nc.psum_tensor(f"ps_score{i}", [P, T], F32)) for i in range(2)]
        ps_sum = ctx.enter_context(nc.psum_tensor("ps_sum", [P, T], F32))
        ps_turn = ctx.enter_context(nc.psum_tensor("ps_turn", [P, T], F32))
        turn_h = ps_turn[:, :].bitcast(BF16)

        def max_bank(u):
            return ps_max[u % MAX_BANKS // 2][:, u % 2 * T:(u % 2 + 1) * T]

        consts = sem("consts_b")
        self_loaded = [sem(f"self_loaded{i}") for i in range(2)]
        cross_loaded = [sem(f"cross_loaded{i}") for i in range(2)]
        shift_self = [sem(f"shift_self{i}") for i in range(2)]
        shift_cross = [sem(f"shift_cross{i}") for i in range(2)]
        scores_ready, probs_ready, summed = sem("scores_ready"), sem("probs_ready"), sem("summed")
        unit_ready, unit_max = sem("unit_ready"), sem("unit_max")
        split_step, neg_split = sem("split_step"), sem("neg_split")
        rows_turned, sums_turned = sem("rows_turned"), sem("sums_turned")
        rows_copied, sums_copied = sem("rows_copied"), sem("sums_copied")
        inv_ready, scaled, y_added = sem("inv_ready"), sem("scaled"), sem("y_added")

        pe_passed, pool_passed, sp_passed = sem("pe_passed_b"), sem("pool_passed_b"), sem("sp_passed_b")
        block = ctx.enter_context(nc.Block())

        def groups(eng, group):
            group(0, 0, 1, False, True)
            with eng.Fori(0, (NG - 2) // 2) as i:
                group(i * 2 + 1, 1, i + 1, True, True)
                group(i * 2 + 2, 0, i + 2, True, True)
            group(NG - 1, 1, NG // 2, True, False)

        @block.sync
        def _(sp):
            def load_stack_q(dst, src, n, loaded):
                rows = src.rearrange("b (g j) p d t -> (b g) (p d) j t", j=GH)
                at = 0
                for lo, hi in Q_STACK:
                    m = (hi - lo) * D
                    sp.dma_start(dst[at:at + m], rows[n, lo * D:hi * D]).then_inc(loaded, 16)
                    at += m

            def load_stack_k(dst, src, n, loaded):
                rows = src.rearrange("b (g j) p d t -> (b g) (p d) j t", j=GH)
                for r, p in enumerate(K_STACK):
                    sp.dma_start(dst[r * D:(r + 1) * D], rows[n, p * D:(p + 1) * D]).then_inc(loaded, 16)

            def load_self(n, s):
                load_stack_q(q_self[s], scr["q"], n, self_loaded[s])
                load_stack_k(k_self[s], scr["k"], n, self_loaded[s])

            def load_cross(n, s):
                load_stack_q(q_cross[s], scr["qc"], n, cross_loaded[s])
                load_stack_k(k_cross[s], scr["kc"], n, cross_loaded[s])
                sp.dma_start(values[s][:, :, :], scr["v"].rearrange("b g p k f -> (b g) p k f")[n])\
                  .then_inc(cross_loaded[s], 16)

            for n in range(2):
                load_self(n, n)
                load_cross(n, n)
            a, w_gate, w_down, experts_loaded = experts

            def load_weights(e, which):
                w, name = ((w_gate, "gating_w"), (w_down, "linear_w"))[which]
                m = w.shape[1] // E
                sp.dma_start(w[:, bass.ds(e * m, m)], a[name][:, bass.ds(e * m, m)]).then_inc(experts_loaded, 16)

            with sp.Fori(0, (NG - 2) // 2) as i:
                for s in range(2):
                    n = i * 2 + s
                    reached_apart(sp, summed, n * STEPS + KS, sp_passed)
                    load_self(n + 2, s)
                    reached_apart(sp, summed, n * STEPS + STEPS, sp_passed)
                    load_cross(n + 2, s)
                    load_weights(i, s)
            for which in range(2):
                load_weights(E - 1, which)

        @block.gpsimd
        def _(pool):
            pool.memset(ident[:, :], 0.0).then_inc(split_step, 1)
            pool.memset(ident_h[:, :], 0.0).then_inc(split_step, 1)
            pool.memset(mask_q[:, :], 0.0).then_inc(split_step, 1)
            pool.memset(mask_k[:, :], 0.0).then_inc(split_step, 1)
            pool.wait_ge(split_step, 4)
            for t in (ident, ident_h):
                pool.affine_select(out=t[:, :], in_=t[:, :], compare_op=ALU.not_equal, fill=1.0,
                                   base=0, pattern=[[-1, P]], channel_multiplier=1).then_inc(consts, 1)
            pool.affine_select(out=mask_q[:, :], in_=mask_q[:, :], compare_op=ALU.is_ge, fill=MASKED,
                               base=0, pattern=[[-1, P]], channel_multiplier=1).then_inc(consts, 1)
            pool.affine_select(out=mask_k[:, :], in_=mask_k[:, :], compare_op=ALU.is_ge, fill=MASKED,
                               base=0, pattern=[[1, P]], channel_multiplier=-1).then_inc(consts, 1)

            def split_maxima(kind, n):
                at = (n * 2 + kind) * 3 + 4
                nm, rest, parts = neg_max[kind], neg_rest[kind], neg_parts[kind]
                reached_apart(pool, unit_max, n * UNITS + SELF_UNITS * (kind + 1), pool_passed)
                pool.tensor_copy(parts[:, 0, :], nm[:, :]).then_inc(split_step, 1)
                pool.wait_ge(split_step, at + 1)
                pool.tensor_tensor(rest[:, :], nm[:, :], parts[:, 0, :], ALU.subtract).then_inc(split_step, 1)
                reached_apart(pool, split_step, at + 2, pool_passed)
                pool.tensor_copy(parts[:, 1, :], rest[:, :]).then_inc(split_step, 1)
                pool.wait_ge(split_step, at + 3)
                pool.tensor_tensor(parts[:, 2, :], rest[:, :], parts[:, 1, :], ALU.subtract).then_inc(neg_split, 1)

            def send_rows(kind, n, slot):
                stack = (q_self, q_cross)[kind][slot]
                reached_apart(pool, rows_copied, n * 2 + kind + 1, pool_passed)
                pool.dma_start(stack[PAIR_ROWS:PAIR_ROWS + SHIFT_ROWS].rearrange("p j t -> p (j t)"),
                               shift_rows[kind][:, :]).then_inc((shift_self, shift_cross)[kind][slot], 16)

            def add_cross(n):
                pool.wait_ge(scaled, n * 2 + 2)
                y = y_all[:, n, :, :]
                pool.tensor_tensor(y, y, y_cross[:, :, :, :].rearrange("p q j d -> p q (j d)"), ALU.add)\
                    .then_inc(y_added, 1)

            def group(n, slot, k, prev, nxt):
                send_rows(1, n, slot)
                if prev:
                    add_cross(n - 1)
                if nxt:
                    split_maxima(0, n + 1)
                    send_rows(0, n + 1, 1 - slot)
                    split_maxima(1, n + 1)

            split_maxima(0, 0)
            send_rows(0, 0, 0)
            split_maxima(1, 0)
            groups(pool, group)
            add_cross(NG - 1)

        @block.scalar
        def _(act):
            def copy_rows(kind, n):
                act.wait_ge(rows_turned, n * 2 + kind + 1)
                act.activation(shift_rows[kind][:, :], turn_h[0:ROWS, 0:P], ACT.Copy).then_inc(rows_copied, 1)

            def copy_sums(kind, n):
                act.wait_ge(summed, n * STEPS + (STEPS if kind else KS))
                act.activation(sums[kind][:, :], ps_sum[:, :], ACT.Copy).then_inc(sums_copied, 1)

            def group(n, slot, k, prev, nxt):
                for step in range(STEPS):
                    off = step * P if step < KS else 0
                    reached(act, summed, n * STEPS + step - 1)
                    for h in range(GH):
                        g = (n * STEPS + step) * GH + h
                        act.wait_ge(scores_ready, g + 1)
                        act.activation(probs[step % 2][:, h, off:T], ps_score[h % 2][:, off:T], ACT.Exp, scale=SCALE)\
                           .then_inc(probs_ready, 1)
                    if step == 0:
                        copy_rows(1, n)
                        if prev:
                            copy_sums(1, n - 1)
                    if step == KS:
                        copy_sums(0, n)
                    if step == KS + 4 and nxt:
                        copy_rows(0, n + 1)

            copy_rows(0, 0)
            groups(act, group)
            copy_sums(1, NG - 1)

        @block.vector
        def _(dve):
            def units(n, us):
                for u in us:
                    h, t = divmod(u % SELF_UNITS, QT)
                    kind = u // SELF_UNITS
                    scores = ps_max[u % 2][:, :] if kind else max_bank(u)[:, 0:(t + 1) * P]
                    dve.wait_ge(unit_ready, n * UNITS + u + 1)
                    dve.tensor_reduce(neg_max[kind][:, h * QT + t:h * QT + t + 1], scores,
                                      AX.X, ALU.max, negate=True).then_inc(unit_max, 1)

            def normalise(kind, n):
                t = ps_turn[:, :].rearrange("p (q j f) -> p q j f", q=QT, j=GH)
                v = inv[kind][:, :].rearrange("p (q j f) -> p q j f", q=QT, j=GH)
                dve.wait_ge(sums_turned, n * 2 + kind + 1)
                dve.reciprocal(v, t[:, :, :, 0:1]).then_inc(inv_ready, 1)
                dve.wait_ge(inv_ready, n * 2 + kind + 1)
                if kind:
                    reached(dve, y_added, n)
                    out = y_cross[:, :, :, :]
                else:
                    out = y_all[:, n, :, :].rearrange("p q (j d) -> p q j d", j=GH)
                dve.tensor_tensor(out, t[:, :, :, 1:1 + D], v.to_broadcast([P, QT, GH, D]), ALU.mult)\
                   .then_inc(scaled, 1)

            def group(n, slot, k, prev, nxt):
                for step in range(STEPS):
                    if nxt:
                        units(n + 1, units_of_step(step))
                    if step == 1 and prev:
                        normalise(1, n - 1)
                    if step == KS + 2:
                        normalise(0, n)

            units(0, range(SELF_UNITS))
            for t in k_self + k_cross:
                dve.memset(t[PAIR_ROWS:P].rearrange("p j t -> p (j t)").bitcast(F32), PAIR_OF_ONES).then_inc(consts, 1)
            units(0, range(SELF_UNITS, UNITS))
            groups(dve, group)
            normalise(1, NG - 1)

        @block.tensor
        def _(pe):
            def unit(n, u, slot):
                h, t = divmod(u % SELF_UNITS, QT)
                q = (q_self, q_cross)[u // SELF_UNITS][slot][0:PAIR_ROWS, h, t * P:(t + 1) * P]
                if u < SELF_UNITS:
                    reached(pe, unit_max, n * UNITS + (u - 3 if u >= MAX_BANKS else u // 2 - 1))
                    out = max_bank(u)
                    pe.matmul(out[:, 0:(t + 1) * P], q, k_self[slot][0:PAIR_ROWS, h, 0:(t + 1) * P],
                              start=True, stop=False)
                    pe.matmul(out[:, t * P:(t + 1) * P], ident_h[:, :], mask_q[:, :],
                              start=False, stop=True).then_inc(unit_ready, 1)
                    return
                before = u - SELF_UNITS
                reached(pe, unit_max, n * UNITS + (u - 1 if before >= 2 else SELF_UNITS - 2 + 2 * before))
                for c in range(TC // T):
                    ins = pe.matmul(ps_max[u % 2][:, c * T:(c + 1) * T], q,
                                    k_cross[slot][0:PAIR_ROWS, h, c * T:(c + 1) * T], start=True, stop=True)
                ins.then_inc(unit_ready, 1)

            def scores(n, step, h, slot):
                g = (n * STEPS + step) * GH + h
                reached(pe, probs_ready, g - 1)
                last = PAIR_ROWS + SHIFT_ROWS
                out = ps_score[h % 2]
                if step < KS:
                    off = step * P
                    pe.matmul(out[:, off:T], k_self[slot][0:last, h, off:off + P], q_self[slot][0:last, h, off:T],
                              start=True, stop=False)
                    ins = pe.matmul(out[:, off:off + P], ident_h[:, :], mask_k[:, :], start=False, stop=True)
                else:
                    off = (step - KS) * P
                    ins = pe.matmul(out[:, :], k_cross[slot][0:last, h, off:off + P], q_cross[slot][0:last, h, :],
                                    start=True, stop=True)
                ins.then_inc(scores_ready, 1)

            def weigh(n, step, slot):
                off = step * P if step < KS else 0
                first = step in (0, KS)
                last = step in (KS - 1, STEPS - 1)
                if first:
                    reached(pe, sums_copied, n * 2 + (1 if step else 0))
                pe.wait_ge(probs_ready, (n * STEPS + step + 1) * GH)
                for h in range(GH):
                    ins = pe.matmul(ps_sum[h * VW:(h + 1) * VW, off:T], values[slot][:, step, h * VW:(h + 1) * VW],
                                    probs[step % 2][:, h, off:T], start=first, stop=last, tile_position=(0, h * VW))
                ins.then_inc(summed, 1)

            def turn_rows(kind, n):
                if kind:
                    pe.wait_ge(rows_copied, n * 2 + 1)
                else:
                    reached(pe, scaled, n * 2 - 1)
                reached_apart(pe, neg_split, n * 2 + kind + 1, pe_passed)
                pe.transpose(turn_h[0:ROWS, 0:P], neg_parts[kind][:, :, :].rearrange("p s j -> p (s j)"),
                             ident_h[:, :]).then_inc(rows_turned, 1)

            def turn_sums(kind, n):
                if kind:
                    if not (isinstance(n, int) and n == NG - 1):
                        pe.wait_ge(rows_copied, n * 2 + 4)
                    else:
                        pe.wait_ge(scaled, n * 2 + 1)
                else:
                    pe.wait_ge(rows_copied, n * 2 + 2)
                    reached(pe, scaled, n * 2)
                pe.wait_ge(sums_copied, n * 2 + kind + 1)
                for t in range(QT):
                    ins = pe.transpose(ps_turn[:, t * P:(t + 1) * P], sums[kind][:, t * P:(t + 1) * P], ident[:, :])
                ins.then_inc(sums_turned, 1)

            def group(n, slot, k, prev, nxt):
                for step in range(STEPS):
                    if step == 0:
                        pe.wait_ge(shift_self[slot], k * 16)
                        if nxt:
                            pe.wait_ge(self_loaded[1 - slot], (k + (slot == 1)) * LOAD_A)
                    if step == KS:
                        pe.wait_ge(shift_cross[slot], k * 16)
                        if nxt:
                            pe.wait_ge(cross_loaded[1 - slot], (k + (slot == 1)) * LOAD_B)
                    if not nxt:
                        fill = ((), (), (), ())
                    elif step < KS:
                        fill = tuple((u,) for u in units_of_step(step))
                    else:
                        u0, u1 = units_of_step(step)
                        fill = ((u0,), (), (u1,), ())
                    for h in range(GH):
                        scores(n, step, h, slot)
                        for u in fill[h]:
                            unit(n + 1, u, 1 - slot)
                        if h == 1 and step:
                            weigh(n, step - 1, slot)
                        elif h == 1 and prev:
                            weigh(n - 1, STEPS - 1, 1 - slot)
                    if step == 0:
                        turn_rows(1, n)
                    elif step == KS + 4 and nxt:
                        turn_rows(0, n + 1)
                    if step == 1 and prev:
                        turn_sums(1, n - 1)
                    if step == KS + 2:
                        turn_sums(0, n)

            pe.wait_ge(consts, 4)
            pe.wait_ge(self_loaded[0], LOAD_A)
            for u in range(SELF_UNITS):
                unit(0, u, 0)
            turn_rows(0, 0)
            pe.wait_ge(cross_loaded[0], LOAD_B)
            for u in range(SELF_UNITS, UNITS):
                unit(0, u, 0)
            pe.wait_ge(consts, 8)
            groups(pe, group)
            weigh(NG - 1, STEPS - 1, (NG - 1) % 2)
            turn_sums(1, NG - 1)


 
TOPK = 2
HID = 512
HC = HID // P
NT = B * T // P
SLOT_TILES = NT * TOPK + E - 1
DUMP = B * T


def build_router_inputs(nc, a, y_all, x2_rows, out_rows, logits):
    with ExitStack() as ctx:
        def sb(name, shape, dt=F32):
            return ctx.enter_context(nc.sbuf_tensor(name, shape, dt))

        def sem(name):
            return ctx.enter_context(nc.semaphore(name))

        wp = sb("wp", [P, CH, C])
        wr = sb("wr", [P, CH, E])
        wr_scaled = sb("wr_scaled", [P, CH, E])
        router_scale = sb("router_scale", [P, CH])
        bp_row = sb("bp_row", [P, C])
        zero_rows = sb("zero_rows", [P, C])
        ident = sb("ident_c", [P, P])
        x1 = sb("x1", [P, NT, C])
        y_in = [sb(f"y_in{i}", [P, QT, C]) for i in range(2)]
        x2 = [sb(f"x2_{i}", [P, QT, C]) for i in range(2)]
        turned = [sb(f"turned{i}", [P, CH, T]) for i in range(2)]
        squares = sb("squares", [P, C])
        stats = sb("stats_c", [P, QT, 6])
        mean_var = sb("mean_var_c", [P, NT, 2])
        square_sum = sb("square_sum", [P, NT])
        rstd = sb("rstd_c", [P, NT])
        rms = sb("rms_c", [P, NT])
        rms_scaled = sb("rms_scaled", [P, NT])
        root = sb("root_c", [P, 3, NT])
        ps_T = [ctx.enter_context(nc.psum_tensor(f"ps_T{i}", [P, T], F32)) for i in range(CH)]
        ps_o = [[ctx.enter_context(nc.psum_tensor(f"ps_proj{s}{i}", [P, 2, C], F32)) for i in range(QT // 2)]
                for s in range(2)]
        ps_l = ctx.enter_context(nc.psum_tensor("ps_logits", [P, NT, E], F32))

        loaded, consts, wr_ready = sem("loaded_c"), sem("consts_c"), sem("wr_ready")
        x_loaded = [sem(f"x_loaded_c{i}") for i in range(2)]
        y_copied, T_ready, T_copied = sem("y_copied"), sem("T_ready"), sem("T_copied")
        products, x_biased, x1_ready = sem("products_c"), sem("x_biased"), sem("x1_ready")
        ln_step, root_ready, x2_ready = sem("ln_step_c"), sem("root_c_ready"), sem("x2_ready")
        squared, logits_ready = sem("squared"), sem("logits_ready")
        x1_stored, spare_stored = sem("x1_stored"), sem("spare_stored")
        x2_stored = [sem(f"x2_stored{i}") for i in range(2)]
        N_LOADS = 4
        ROWS_STEPS = 2 * QT

        sp_passed = sem("sp_passed_c")
        block = ctx.enter_context(nc.Block())

        def batches(eng, body):
            with eng.Fori(0, B // 2) as i:
                for s in range(2):
                    body(i * 2 + s, s, i + 1)

        @block.sync
        def _(sp):
            for b in range(B):
                reached(sp, x_loaded[b % 2], b // 2 * 16)
                sp.dma_start(x1[:, b * QT:(b + 1) * QT, :], a["x"][b].rearrange("(j p) c -> p j c", p=P))\
                  .then_inc(x_loaded[b % 2], 16)
                if b == 0:
                    sp.dma_start(wp[:, :, :], a["Wp"].rearrange("(c p) n -> p c n", p=P)).then_inc(loaded, 16)
                    sp.dma_start(wr[:, :, :], a["router_w"].rearrange("(c p) e -> p c e", p=P)).then_inc(loaded, 16)
                    sp.dma_start(router_scale[:, :], a["router_scale"]).then_inc(loaded, 16)
                    sp.dma_start(bp_row[:, :], a["bp"].rearrange("(o n) -> o n", o=1).to_broadcast([P, C]))\
                      .then_inc(loaded, 16)
            sp.wait_ge(consts, 3)
            for rows in (x2_rows, out_rows):
                sp.dma_start(rows[DUMP:DUMP + P], zero_rows[:, :]).then_inc(spare_stored, 16)

            def store_x1(b, s, k):
                reached_apart(sp, x1_ready, b + 1 + 2, sp_passed)
                sp.dma_start(out_rows[bass.ds(b * T, T)].rearrange("(j p) c -> p j c", p=P),
                             x1[:, bass.ds(b * QT, QT), :]).then_inc(x1_stored, 16)

            def store_x2(b, s, k):
                reached_apart(sp, x2_ready, b + 1, sp_passed)
                sp.dma_start(x2_rows[bass.ds(b * T, T)].rearrange("(j p) c -> p j c", p=P), x2[s][:, :, :])\
                  .then_inc(x2_stored[s], 16)

            batches(sp, store_x1)
            batches(sp, store_x2)
            sp.wait_ge(spare_stored, 16 * 2)
            sp.wait_ge(x1_stored, 16 * B)
            for s in range(2):
                sp.wait_ge(x2_stored[s], 16 * (B // 2 + 1))

        @block.gpsimd
        def _(pool):
            pool.memset(ident[:, :], 0.0).then_inc(consts, 1)
            pool.memset(zero_rows[:, :], 0.0).then_inc(consts, 1)
            pool.wait_ge(consts, 2)
            pool.affine_select(out=ident[:, :], in_=ident[:, :], compare_op=ALU.not_equal, fill=1.0,
                               base=0, pattern=[[-1, P]], channel_multiplier=1).then_inc(consts, 1)

            pool.wait_ge(loaded, 16 * N_LOADS)

            def add_bias(b, s, k):
                pool.wait_ge(x_loaded[s], k * 16)
                rows = x1[:, bass.ds(b * QT, QT), :]
                pool.tensor_tensor(rows, rows, bp_row[:, :].rearrange("p (o c) -> p o c", o=1).to_broadcast([P, QT, C]),
                                   ALU.add).then_inc(x_biased, 1)

            batches(pool, add_bias)

        @block.scalar
        def _(act):
            act.sem_inc(T_copied, CH)

            def copy_turned(n, s, k):
                for c in range(CH):
                    act.wait_ge(T_ready, n * CH + c + 1 + 2 * CH)
                    act.wait_ge(products, 2 * n + 2)
                    act.activation(turned[s][:, c, :], ps_T[c][:, :], ACT.Identity).then_inc(T_copied, 1)

            with act.Fori(0, B // 2) as i:
                for s in range(2):
                    b = i * 2 + s
                    act.wait_ge(T_ready, b * CH + CH)
                    act.activation(y_in[s][:, :, :].rearrange("p q (g f) -> p g q f", g=H // GH),
                                   y_all[:, bass.ds(b * (H // GH), H // GH), :, :], ACT.Identity).then_inc(y_copied, 1)
                for s in range(2):
                    copy_turned(i * 2 + s, s, i + 1)
            act.wait_ge(ln_step, B * ROWS_STEPS + 1)
            act.activation(root[:, 1, :], root[:, 0, :], ACT.Sqrt).then_inc(root_ready, 1)
            batches(act, lambda b, s, k: copy_turned(b + B, s, k))
            act.wait_ge(ln_step, B * ROWS_STEPS + ROOT_STEPS + 1)
            act.activation(root[:, 1, :], root[:, 0, :], ACT.Sqrt).then_inc(root_ready, 1)

        @block.vector
        def _(dve):
            for q in x2_stored:
                dve.sem_inc(q, 16)
            dve.sem_inc(x1_ready, 2)
            dve.sem_inc(squared, 1)
            dve.wait_ge(loaded, 16 * N_LOADS)
            for c in range(CH):
                dve.tensor_scalar(wr_scaled[:, c, :], wr[:, c, :], router_scale[:, c:c + 1], None, ALU.mult)\
                   .then_inc(wr_ready, 1)

            def add_and_measure(b, s, k):
                dve.wait_ge(x_biased, b + 1)
                for i in range(QT // 2):
                    dve.wait_ge(products, 2 * b + i + 1 + 4)
                    rows = x1[:, b * QT + 2 * i:b * QT + 2 * i + 2, :]
                    ins = dve.tensor_tensor(rows, ps_o[s][i][:, :, :], rows, ALU.add)
                ins.then_inc(x1_ready, 1)
                dve.wait_ge(x1_ready, b + 1 + 2)
                for j in range(QT):
                    dve.bn_stats(stats[:, j, :], x1[:, b * QT + j, :]).then_inc(ln_step, 1)
                for j in range(QT):
                    dve.wait_ge(ln_step, b * ROWS_STEPS + j + 1)
                    dve.bn_aggr(mean_var[:, b * QT + j, :], stats[:, j, :]).then_inc(ln_step, 1)

            def norm(b, s, k):
                dve.wait_ge(x2_stored[s], k * 16)
                dve.wait_ge(T_ready, (b + B) * CH + CH)
                for j in range(QT):
                    t = b * QT + j
                    ins = dve.tensor_scalar(x2[s][:, j, :], x1[:, t, :], mean_var[:, t, 0:1], rstd[:, t:t + 1],
                                            ALU.subtract, ALU.mult)
                ins.then_inc(x2_ready, 1)
                dve.wait_ge(x2_ready, b + 1)
                for j in range(QT):
                    dve.wait_ge(squared, b * QT + j + 1)
                    dve.tensor_tensor_reduce(squares[:, :], x2[s][:, j, :], x2[s][:, j, :], 1.0, 0.0, ALU.mult,
                                             ALU.add, square_sum[:, b * QT + j:b * QT + j + 1]).then_inc(squared, 1)

            for b in range(B):
                add_and_measure(b, b % 2, b // 2 + 1)
            inverse_root(dve, mean_var[:, :, 1], LN_EPS, root, rstd[:, :], ln_step, B * ROWS_STEPS, root_ready, 1)
            for b in range(B):
                norm(b, b % 2, b // 2 + 1)
            dve.wait_ge(squared, NT + 1)
            inverse_root(dve, square_sum[:, :], RMS_EPS, root, rms[:, :], ln_step, B * ROWS_STEPS + ROOT_STEPS,
                         root_ready, 2, scale=1.0 / C)
            dve.tensor_scalar(rms_scaled[:, :], rms[:, :], float(C) ** -0.5, None, ALU.mult).then_inc(logits_ready, 1)
            dve.wait_ge(logits_ready, 1)
            dve.wait_ge(products, 4 * B + 4)
            dve.tensor_tensor(logits[:, :, :], ps_l[:, :, :],
                              rms_scaled[:, :].rearrange("p (i o) -> p i o", o=1).to_broadcast([P, NT, E]), ALU.mult)\
               .then_inc(logits_ready, 1)

        @block.tensor
        def _(pe):
            pe.sem_inc(T_ready, 2 * CH)
            pe.sem_inc(products, 4)
            pe.wait_ge(consts, 3)

            def turn(src, n):
                for c in range(CH):
                    pe.wait_ge(T_copied, n * CH + c + 1)
                    for j in range(QT):
                        ins = pe.transpose(ps_T[c][:, j * P:(j + 1) * P], src[:, j, c * P:(c + 1) * P], ident[:, :])
                    ins.then_inc(T_ready, 1)

            def multiply(out, n, s, weights):
                pe.wait_ge(T_copied, (n + 2) * CH)
                for j in range(QT):
                    for c in range(CH):
                        ins = pe.matmul(out(j), turned[s][:, c, j * P:(j + 1) * P], weights[:, c, :],
                                        start=(c == 0), stop=(c == CH - 1))
                    if j % 2:
                        ins.then_inc(products, 1)

            with pe.Fori(0, B // 2) as i:
                for s in range(2):
                    pe.wait_ge(y_copied, i * 2 + s + 1)
                    turn(y_in[s], i * 2 + s)
                pe.wait_ge(loaded, 16 * N_LOADS)
                for s in range(2):
                    pe.wait_ge(x1_ready, i * 2 + s + 1)
                    multiply(lambda j: ps_o[s][j // 2][:, j % 2, :], i * 2 + s, s, wp)
            pe.wait_ge(wr_ready, CH)
            with pe.Fori(0, B // 2) as i:
                for s in range(2):
                    pe.wait_ge(x2_ready, i * 2 + s + 1)
                    turn(x2[s], i * 2 + s + B)
                for s in range(2):
                    multiply(lambda j: ps_l[:, bass.ds((i * 2 + s) * QT + j, 1), :].rearrange("p o e -> p (o e)"),
                             i * 2 + s + B, s, wr_scaled)


LOWEST = -3.0e38
WHOLE = 1.5 * 2.0 ** 23


def build_routing(nc, a, logits, slot_row, slot_weight, tile_expert):
    with ExitStack() as ctx:
        def sb(name, shape, dt=F32):
            return ctx.enter_context(nc.sbuf_tensor(name, shape, dt))

        def sem(name):
            return ctx.enter_context(nc.semaphore(name))

        top = sb("top", [P, NT])
        shifted = sb("shifted", [P, NT, E])
        probs = sb("probs_d", [P, NT, E])
        total = sb("total", [P, NT])
        others = sb("others", [P, NT, E])
        chosen = [sb(f"chosen{k}", [P, NT, E]) for k in range(TOPK)]
        either = sb("either", [P, NT, E])
        either_h = sb("either_h", [P, NT, E], BF16)
        weight_all = sb("weight_all", [P, NT, E])
        work = sb("work", [P, NT, E])
        weight = [sb(f"weight{k}", [P, NT]) for k in range(TOPK)]
        place = sb("place", [P, NT, E])
        place_k = sb("place_k", [P, NT])
        lo = [sb(f"lo{k}", [P, NT]) for k in range(TOPK)]
        hi = [sb(f"hi{k}", [P, NT]) for k in range(TOPK)]
        count = sb("count", [P, E])
        over = sb("over", [P, E, NT])
        tiles = sb("tiles", [P, E])
        before = sb("before", [P, E, E])
        first_tile = sb("first_tile", [P, E])
        end_tile = sb("end_tile", [P, E])
        ended = sb("ended", [P, SLOT_TILES, E])
        expert_f = sb("expert_f", [P, SLOT_TILES])
        per_expert = sb("per_expert", [P, E])
        lo_onehot = [sb(f"lo_onehot{k}", [P, NT, P]) for k in range(TOPK)]
        hi_onehot = sb("hi_onehot", [P, NT, SLOT_TILES])
        hi_values = [sb(f"hi_values{k}", [P, NT, 2, SLOT_TILES]) for k in range(TOPK)]
        row_plus = sb("row_plus", [P, SLOT_TILES])
        empty = sb("empty", [P, SLOT_TILES])
        lower = sb("lower", [P, E, E])
        earlier = sb("earlier", [P, P], BF16)
        ones_h = sb("ones_h", [P, P], BF16)
        tile_128 = sb("tile_128", [P, NT])
        slot_tile = sb("slot_tile", [P, SLOT_TILES])
        order = sb("order", [P, E])
        column = sb("column", [P, P])
        token = sb("token", [P, NT])
        dump = sb("dump", [P, 1])
        ps_place = ctx.enter_context(nc.psum_tensor("ps_place", [P, NT, E], F32))
        ps_count = ctx.enter_context(nc.psum_tensor("ps_count", [P, NT, E], F32))
        ps_slots = ctx.enter_context(nc.psum_tensor("ps_slots", [P, 2, SLOT_TILES], F32))

        loaded, consts, step = sem("loaded_d"), sem("consts_d"), sem("step_d")
        shifted_ready, exp_ready = sem("shifted_ready"), sem("exp_ready")
        either_ready, placed, onehot_ready, slots_ready = sem("either_ready"), sem("placed"), sem("onehot_ready"), sem("slots_ready")
        N_CONSTS = 11

        block = ctx.enter_context(nc.Block())

        @block.sync
        def _(sp):
            sp.dma_start(per_expert[:, :], a["per_expert_scale"].rearrange("(o n) -> o n", o=1).to_broadcast([P, E]))\
              .then_inc(loaded, 16)

        @block.gpsimd
        def _(pool):
            done = [0]

            def const(ins):
                done[0] += 1
                ins.then_inc(consts, 1)
                pool.wait_ge(consts, done[0])

            const(pool.memset(lower[:, :, :], 1.0))
            const(pool.affine_select(out=lower[:, :, :], in_=lower[:, :, :], compare_op=ALU.is_gt, fill=0.0,
                                     base=0, pattern=[[1, E], [-1, E]], channel_multiplier=0))
            const(pool.memset(earlier[:, :], 1.0))
            const(pool.affine_select(out=earlier[:, :], in_=earlier[:, :], compare_op=ALU.is_gt, fill=0.0,
                                     base=0, pattern=[[1, P]], channel_multiplier=-1))
            const(pool.memset(ones_h[:, :], 1.0))
            for t, pattern, base, per_row in ((tile_128, [[P, NT]], 0, 0), (slot_tile, [[1, SLOT_TILES]], 0, 0),
                                              (order, [[-1, E]], E, 0), (column, [[1, P]], 0, 0),
                                              (token, [[P, NT]], 1, 1), (dump, [[0, 1]], DUMP + 1, 1)):
                const(pool.iota(t[:, :], pattern, base=base, channel_multiplier=per_row,
                                allow_small_or_imprecise_dtypes=True))
            assert done[0] == N_CONSTS

        @block.scalar
        def _(act):
            act.wait_ge(shifted_ready, 1)
            act.activation(probs[:, :, :], shifted[:, :, :], ACT.Exp).then_inc(exp_ready, 1)

        @block.vector
        def _(dve):
            done = [0]

            def link(ins):
                done[0] += 1
                ins.then_inc(step, 1)
                dve.wait_ge(step, done[0])

            def along(t, n):
                return t[:, :].rearrange("p (i o) -> p i o", o=1).to_broadcast([P, NT, n])

            def per_tile(t, n):
                return t[:, :].rearrange("p (o e) -> p o e", o=1).to_broadcast([P, NT, n])

            full = [P, NT, E]
            link(dve.tensor_reduce(top[:, :], logits[:, :, :], AX.X, ALU.max))
            dve.tensor_tensor(shifted[:, :, :], logits[:, :, :], along(top, E), ALU.subtract).then_inc(shifted_ready, 1)
            dve.wait_ge(consts, N_CONSTS)
            link(dve.tensor_tensor(work[:, :, :], logits[:, :, :], along(top, E), ALU.is_equal))
            for k in range(TOPK):
                link(dve.tensor_tensor(work[:, :, :], work[:, :, :], per_tile(order, E), ALU.mult))
                link(dve.tensor_reduce(top[:, :], work[:, :, :], AX.X, ALU.max))
                link(dve.tensor_tensor(chosen[k][:, :, :], work[:, :, :], along(top, E), ALU.is_equal))
                if k == 0:
                    link(dve.scalar_tensor_tensor(others[:, :, :], chosen[0][:, :, :], LOWEST, logits[:, :, :],
                                                  ALU.mult, ALU.add))
                    link(dve.tensor_reduce(top[:, :], others[:, :, :], AX.X, ALU.max))
                    link(dve.tensor_tensor(work[:, :, :], others[:, :, :], along(top, E), ALU.is_equal))
            dve.tensor_tensor(either_h[:, :, :], chosen[0][:, :, :], chosen[1][:, :, :], ALU.add).then_inc(either_ready, 1)
            link(dve.tensor_tensor(either[:, :, :], chosen[0][:, :, :], chosen[1][:, :, :], ALU.add))
            dve.wait_ge(loaded, 16)
            dve.wait_ge(exp_ready, 1)
            link(dve.tensor_reduce(total[:, :], probs[:, :, :], AX.X, ALU.add))
            link(dve.reciprocal(total[:, :], total[:, :]))
            link(dve.tensor_tensor(probs[:, :, :], probs[:, :, :], along(total, E), ALU.mult))
            link(dve.tensor_tensor(work[:, :, :], probs[:, :, :], either[:, :, :], ALU.mult))
            link(dve.tensor_reduce(total[:, :], work[:, :, :], AX.X, ALU.add))
            link(dve.tensor_scalar(top[:, :], total[:, :], 0.0, None, ALU.is_le))
            link(dve.tensor_tensor(total[:, :], total[:, :], top[:, :], ALU.add))
            link(dve.reciprocal(total[:, :], total[:, :]))
            link(dve.tensor_tensor(weight_all[:, :, :], probs[:, :, :], along(total, E), ALU.mult))
            link(dve.tensor_tensor(weight_all[:, :, :], weight_all[:, :, :], per_tile(per_expert, E), ALU.mult))
            for k in range(TOPK):
                link(dve.tensor_tensor(work[:, :, :], weight_all[:, :, :], chosen[k][:, :, :], ALU.mult))
                link(dve.tensor_reduce(weight[k][:, :], work[:, :, :], AX.X, ALU.add))
            dve.wait_ge(placed, 1)
            link(dve.tensor_reduce(count[:, :], ps_count[:, :, :].rearrange("p i e -> p e i"), AX.X, ALU.add))
            link(dve.tensor_tensor(over[:, :, :], count[:, :].rearrange("p (e o) -> p e o", o=1).to_broadcast([P, E, NT]),
                                   tile_128[:, :].rearrange("p (o i) -> p o i", o=1).to_broadcast([P, E, NT]), ALU.is_gt))
            link(dve.tensor_reduce(tiles[:, :], over[:, :, :], AX.X, ALU.add))
            link(dve.tensor_tensor(before[:, :, :], lower[:, :, :],
                                   tiles[:, :].rearrange("p (o f) -> p o f", o=1).to_broadcast([P, E, E]), ALU.mult))
            link(dve.tensor_reduce(first_tile[:, :], before[:, :, :], AX.X, ALU.add))
            link(dve.tensor_tensor(end_tile[:, :], first_tile[:, :], tiles[:, :], ALU.add))
            link(dve.tensor_scalar(first_tile[:, :], first_tile[:, :], float(P), None, ALU.mult))
            link(dve.tensor_tensor(place[:, :, :], ps_place[:, :, :], per_tile(first_tile, E), ALU.add))
            for k in range(TOPK):
                link(dve.tensor_tensor(work[:, :, :], place[:, :, :], chosen[k][:, :, :], ALU.mult))
                link(dve.tensor_reduce(place_k[:, :], work[:, :, :], AX.X, ALU.add))
                link(dve.tensor_scalar(hi[k][:, :], place_k[:, :], 1.0 / P, -0.5 + 0.5 / P, ALU.mult, ALU.add))
                link(dve.tensor_scalar(hi[k][:, :], hi[k][:, :], WHOLE, None, ALU.add))
                link(dve.tensor_scalar(hi[k][:, :], hi[k][:, :], -WHOLE, None, ALU.add))
                link(dve.scalar_tensor_tensor(lo[k][:, :], hi[k][:, :], -float(P), place_k[:, :], ALU.mult, ALU.add))
                dve.tensor_tensor(lo_onehot[k][:, :, :], per_tile(column, P), along(lo[k], P), ALU.is_equal)\
                   .then_inc(onehot_ready, 1)
                link(dve.tensor_tensor(hi_onehot[:, :, :], per_tile(slot_tile, SLOT_TILES), along(hi[k], SLOT_TILES),
                                       ALU.is_equal))
                for v, value in enumerate((token, weight[k])):
                    dve.tensor_tensor(hi_values[k][:, :, v, :], hi_onehot[:, :, :], along(value, SLOT_TILES), ALU.mult)\
                       .then_inc(onehot_ready, 1)
            shape = [P, SLOT_TILES, E]
            link(dve.tensor_tensor(ended[:, :, :],
                                   slot_tile[:, :].rearrange("p (i o) -> p i o", o=1).to_broadcast(shape),
                                   end_tile[:, :].rearrange("p (o e) -> p o e", o=1).to_broadcast(shape), ALU.is_ge))
            link(dve.tensor_reduce(expert_f[:, :], ended[:, :, :], AX.X, ALU.add))
            link(dve.tensor_scalar(tile_expert[:, :], expert_f[:, :], float(E - 1), None, ALU.min))
            dve.wait_ge(slots_ready, 1)
            link(dve.tensor_copy(row_plus[:, :], ps_slots[:, 0, :]))
            link(dve.tensor_copy(slot_weight[:, :], ps_slots[:, 1, :]))
            link(dve.tensor_scalar(empty[:, :], row_plus[:, :], 0.5, dump[:, 0:1], ALU.is_lt, ALU.mult))
            link(dve.tensor_tensor(row_plus[:, :], row_plus[:, :], empty[:, :], ALU.add))
            link(dve.tensor_scalar(slot_row[:, :], row_plus[:, :], -1.0, None, ALU.add))

        @block.tensor
        def _(pe):
            pe.wait_ge(consts, N_CONSTS)
            pe.wait_ge(either_ready, 1)
            pe.matmul(ps_place[:, :, :], earlier[:, :], either_h[:, :, :], start=True, stop=False)
            for i in range(NT - 1):
                n = NT - 1 - i
                pe.matmul(ps_place[:, i + 1:NT, :], ones_h[:, :], either_h[:, i:i + 1, :].to_broadcast([P, n, E]),
                          start=False, stop=(n == 1))
            pe.matmul(ps_count[:, :, :], ones_h[:, :], either_h[:, :, :], start=True, stop=True).then_inc(placed, 1)
            for k in range(TOPK):
                pe.wait_ge(onehot_ready, (k + 1) * 3)
                for i in range(NT):
                    ins = pe.matmul(ps_slots[:, :, :], lo_onehot[k][:, i, :], hi_values[k][:, i, :, :],
                                    start=(k == 0 and i == 0), stop=(k == TOPK - 1 and i == NT - 1))
            ins.then_inc(slots_ready, 1)


def build_experts(nc, x2_rows, out_rows, slot_row, slot_weight, tile_expert, w_gate, w_down,
                  experts_loaded):
    with ExitStack() as ctx:
        def sb(name, shape, dt=F32):
            return ctx.enter_context(nc.sbuf_tensor(name, shape, dt))

        def sem(name):
            return ctx.enter_context(nc.semaphore(name))

        ident = sb("ident_e", [P, P])
        rows_in = sb("rows_in", [P, 2, 1], I32)
        rows_out = sb("rows_out", [P, 2, 1], I32)
        weight_in = sb("weight_in", [P, 2, 1])
        x_in = [sb(f"x_in_e{i}", [P, C]) for i in range(2)]
        xT = [sb(f"xT_e{i}", [P, CH, P]) for i in range(2)]
        gelu = [sb(f"gelu{i}", [P, HID]) for i in range(2)]
        hidden = [sb(f"hidden{i}", [P, HID]) for i in range(2)]
        hiddenT = [sb(f"hiddenT{i}", [P, HC, P]) for i in range(2)]
        y_out = [sb(f"y_out{i}", [P, C]) for i in range(2)]
        ps_gate = [[ctx.enter_context(nc.psum_tensor(f"ps_gate{i}{j}", [P, HID], F32)) for j in range(2)]
                   for i in range(2)]
        ps_xT = ctx.enter_context(nc.psum_tensor("ps_xT_e", [P, CH, P], F32))
        ps_hT = ctx.enter_context(nc.psum_tensor("ps_hT", [P, HC, P], F32))
        ps_y = [ctx.enter_context(nc.psum_tensor(f"ps_y{i}", [P, C], F32)) for i in range(2)]

        consts = sem("consts_e")
        rows_set, rows_back_set = sem("rows_set"), sem("rows_back_set")
        gathered = [sem(f"gathered{i}") for i in range(2)]
        added = sem("added")
        x_turned, x_copied, gates_ready = sem("x_turned"), sem("x_copied"), sem("gates_ready")
        gelu_ready, hidden_ready, h_turned, h_copied = sem("gelu_ready"), sem("hidden_ready"), sem("h_turned"), sem("h_copied")
        down_ready, y_ready = sem("down_ready"), sem("y_ready")

        pool_passed = sem("pool_passed_e")
        block = ctx.enter_context(nc.Block())
        LAST = SLOT_TILES - 1
        assert LAST % 2 == 0

        def each_tile(eng, body):
            body(0, 0, 1)
            body(1, 1, 1)
            with eng.Fori(1, LAST // 2) as i:
                body(i * 2, 0, i + 1)
                body(i * 2 + 1, 1, i + 1)
            body(LAST, 0, LAST // 2 + 1)

        @block.gpsimd
        def _(pool):
            pool.memset(ident[:, :], 0.0).then_inc(consts, 1)
            pool.wait_ge(consts, 1)
            pool.affine_select(out=ident[:, :], in_=ident[:, :], compare_op=ALU.not_equal, fill=1.0,
                               base=0, pattern=[[-1, P]], channel_multiplier=1).then_inc(consts, 1)
            pool.wait_ge(consts, 2)

            def gather(t, s, k):
                reached(pool, x_turned, t - 1)
                reached_apart(pool, gathered[s], k * 16 - 16, pool_passed)
                pool.tensor_copy(rows_in[:, s, :], slot_row[:, bass.ds(t, 1)]).then_inc(rows_set, 1)
                reached_apart(pool, rows_set, t + 1, pool_passed)
                pool.indirect_dma_start(x_in[s][:, :], None, x2_rows, bass.IndirectOffsetOnAxis(rows_in[:, s, :], 0))\
                    .then_inc(gathered[s], 16)

            def add_back(t, s, k):
                reached_apart(pool, added, t * 16, pool_passed)
                pool.tensor_copy(rows_out[:, s, :], slot_row[:, bass.ds(t, 1)]).then_inc(rows_back_set, 1)
                pool.wait_ge(rows_back_set, t + 1)
                reached_apart(pool, y_ready, t + 1, pool_passed)
                pool.indirect_dma_start(out_rows, bass.IndirectOffsetOnAxis(rows_out[:, s, :], 0), y_out[s][:, :], None,
                                        compute_op=ALU.add).then_inc(added, 16)

            gather(0, 0, 1)
            gather(1, 1, 1)
            gather(2, 0, 2)
            gather(3, 1, 2)
            add_back(0, 0, 1)
            with pool.Fori(1, LAST // 2 - 1) as i:
                gather(i * 2 + 2, 0, i + 2)
                add_back(i * 2 - 1, 1, i)
                gather(i * 2 + 3, 1, i + 2)
                add_back(i * 2, 0, i + 1)
            gather(LAST, 0, LAST // 2 + 1)
            for t in range(LAST - 3, LAST + 1):
                add_back(t, t % 2, t // 2 + 1)
            pool.wait_ge(added, SLOT_TILES * 16)

        @block.scalar
        def _(act):
            def tile(t, s, k):
                act.wait_ge(x_turned, t + 1)
                reached(act, gates_ready, (t - 1) * 2)
                act.activation(xT[s][:, :, :], ps_xT[:, :, :], ACT.Copy).then_inc(x_copied, 1)
                act.wait_ge(gates_ready, t * 2 + 1)
                reached(act, hidden_ready, t - 1)
                act.activation(gelu[s][:, :], ps_gate[s][0][:, :], ACT.Gelu_apprx_tanh).then_inc(gelu_ready, 1)

            each_tile(act, tile)

        @block.vector
        def _(dve):
            def tile(t, s, k):
                dve.wait_ge(gelu_ready, t + 1)
                dve.wait_ge(gates_ready, t * 2 + 2)
                reached(dve, h_turned, t - 1)
                dve.tensor_tensor(hidden[s][:, :], ps_gate[s][1][:, :], gelu[s][:, :], ALU.mult)\
                   .then_inc(hidden_ready, 1)
                dve.wait_ge(h_turned, t + 1)
                reached(dve, down_ready, t - 1)
                dve.tensor_copy(hiddenT[s][:, :, :], ps_hT[:, :, :]).then_inc(h_copied, 1)
                dve.wait_ge(down_ready, t + 1)
                reached(dve, added, t * 16 - 16)
                dve.tensor_scalar(y_out[s][:, :], ps_y[s][:, :], slot_weight[:, bass.ds(t, 1)], None, ALU.mult)\
                   .then_inc(y_ready, 1)

            each_tile(dve, tile)

        @block.tensor
        def _(pe):
            def turn_x(t, s, k):
                pe.wait_ge(gathered[s], k * 16)
                reached(pe, x_copied, t)
                for c in range(CH):
                    ins = pe.transpose(ps_xT[:, c, :], x_in[s][:, c * P:(c + 1) * P], ident[:, :])
                ins.then_inc(x_turned, 1)

            def expert(t):
                return pe.value_load(tile_expert[0:1, bass.ds(t, 1)], min_val=0, max_val=E - 1)

            def gate(t, s, j, e):
                if j == 0:
                    pe.wait_ge(x_copied, t + 1)
                    reached(pe, hidden_ready, t - 1)
                for c in range(CH):
                    ins = pe.matmul(ps_gate[s][j][:, :], xT[s][:, c, :],
                                    w_gate[:, bass.ds(e * (CH * 2 * HID) + (c * 2 + j) * HID, HID)],
                                    start=(c == 0), stop=(c == CH - 1))
                ins.then_inc(gates_ready, 1)

            def turn_hidden(t, s, k):
                pe.wait_ge(hidden_ready, t + 1)
                reached(pe, h_copied, t)
                for c in range(HC):
                    ins = pe.transpose(ps_hT[:, c, :], hidden[s][:, c * P:(c + 1) * P], ident[:, :])
                ins.then_inc(h_turned, 1)

            def down(t, s, e):
                pe.wait_ge(h_copied, t + 1)
                reached(pe, y_ready, t - 1)
                for c in range(HC):
                    ins = pe.matmul(ps_y[s][:, :], hiddenT[s][:, c, :],
                                    w_down[:, bass.ds(e * (HC * C) + c * C, C)], start=(c == 0), stop=(c == HC - 1))
                ins.then_inc(down_ready, 1)

            def tile(t, s, k, more=2):
                e_next = expert(t + 1) if more > 0 else None
                e = expert(t)
                if more > 0:
                    gate(t + 1, 1 - s, 0, e_next)
                turn_hidden(t, s, k)
                if more > 1:
                    turn_x(t + 2, s, k + 1)
                if more > 0:
                    gate(t + 1, 1 - s, 1, e_next)
                down(t, s, e)

            pe.wait_ge(consts, 2)
            pe.wait_ge(experts_loaded, 16 * 2 * E)
            turn_x(0, 0, 1)
            e_first = expert(0)
            gate(0, 0, 0, e_first)
            gate(0, 0, 1, e_first)
            turn_x(1, 1, 1)
            tile(0, 0, 1)
            tile(1, 1, 1)
            with pe.Fori(1, LAST // 2 - 1) as i:
                tile(i * 2, 0, i + 1)
                tile(i * 2 + 1, 1, i + 1)
            tile(LAST - 2, 0, LAST // 2)
            tile(LAST - 1, 1, LAST // 2, more=1)
            tile(LAST, 0, LAST // 2 + 1, more=0)


def build_program(nc, a, out_rows):
    scr = {n: nc.dram_tensor(f"scr_{n}", [B, H, NSPLIT, D, TC if n == "kc" else T], BF16).ap()
           for n in ("q", "k", "qc", "kc")}
    scr["v"] = nc.dram_tensor("scr_v", [B, H // GH, P, STEPS, GH * VW], F32).ap()
    x2_rows = nc.dram_tensor("x2_rows", [DUMP + P, C], F32).ap()
    with ExitStack() as ctx:
        def sb(name, shape, dt=F32):
            return ctx.enter_context(nc.sbuf_tensor(name, shape, dt))

        y_all = sb("y_all", [P, NG, QT, GH * D])
        w_gate = sb("w_gate", [P, E * CH * 2 * HID])
        w_down = sb("w_down", [P, E * HC * C])
        logits = sb("logits", [P, NT, E])
        slot_row = sb("slot_row", [P, SLOT_TILES], I32)
        slot_weight = sb("slot_weight", [P, SLOT_TILES])
        tile_expert = sb("tile_expert", [P, SLOT_TILES], I32)
        experts_loaded = ctx.enter_context(nc.semaphore("experts_loaded"))

        build_projections(nc, a, scr)
        build_attention(nc, scr, y_all, (a, w_gate, w_down, experts_loaded))
        build_router_inputs(nc, a, y_all, x2_rows, out_rows, logits)
        build_routing(nc, a, logits, slot_row, slot_weight, tile_expert)
        build_experts(nc, x2_rows, out_rows, slot_row, slot_weight, tile_expert, w_gate, w_down,
                      experts_loaded)


def kernel(**inputs):
    import numpy as np
    import concourse.bacc as bacc
    from concourse.bass_utils import run_bass_kernel_spmd

    def columns(v):
        return v.reshape(-1, P).T

    given = {n.replace("L0_xattn_", "").replace("L0_ffn_", ""): np.asarray(v) for n, v in inputs.items()}
    laid = {n: given[n] for n in ("x", "Wq", "Wk", "Wv", "Wcq", "Wck", "Wcv", "Wp", "bv", "bcv", "bp",
                                  "router_w", "per_expert_scale")}
    laid |= {n: columns(given[n]) for n in ("bq", "bk", "bcq", "bck", "router_scale")}
    laid["ctxT"] = given["ctx_512"].transpose(0, 2, 1)
    laid["gating_w"] = given["gating_w"].reshape(E, 2, HID, CH, P).transpose(4, 0, 3, 1, 2).reshape(P, -1)
    laid["linear_w"] = given["linear_w"].reshape(E, HC, P, C).transpose(2, 0, 1, 3).reshape(P, -1)

    nc = bacc.Bacc("TRN2", target_bir_lowering=False, num_devices=1)
    arrays, args = {}, {}
    for name, v in laid.items():
        v = np.ascontiguousarray(v)
        arrays[f"in_{name}"] = v
        args[name] = nc.dram_tensor(f"in_{name}", v.shape, mybir.dt.from_np(v.dtype), kind="ExternalInput").ap()
    out = nc.dram_tensor("out_rows", [DUMP + P, C], F32, kind="ExternalOutput").ap()
    build_program(nc, args, out)
    r = run_bass_kernel_spmd(nc, [arrays], core_ids=[0])
    return r.results[0]["out_rows"][:DUMP].reshape(B, T, C)
```

```python
from contextlib import ExitStack

import numpy as np
import concourse.bass as bass
from concourse import mybir

F32 = mybir.dt.float32
BF16 = mybir.dt.bfloat16
I32 = mybir.dt.int32
ACT = mybir.ActivationFunctionType
ALU = mybir.AluOpType
AX = mybir.AxisListType

P = 128
B, T, C = 4, 512, 256
TC, CC = 1024, 128
H = 16
D = C // H
CH = C // P
QT = T // P
KS, KC = T // P, TC // P
GH = 4
NG = B * H // GH
VW = 32
E = 8
NSPLIT = 3
PAIR_ROWS = 6 * D
SHIFT_ROWS = NSPLIT
MASKED = -1.0e38
SCALE = float(D) ** -0.5
LN_EPS = 1e-5
RMS_EPS = 1e-6


def reached(eng, sem, count):
    if not (isinstance(count, int) and count <= 0):
        eng.wait_ge(sem, count)


ROOT_STEPS = 6


def root_input(dve, var, eps, root, step, done, scale=1.0):
    dve.wait_ge(step, done)
    dve.tensor_scalar(root[:, 0, :], var, scale, eps, ALU.mult, ALU.add).then_inc(step, 1)


def inverse_of_root(dve, root, out, step, done, root_ready, roots):
    dve.wait_ge(root_ready, roots)
    dve.reciprocal(out, root[:, 1, :]).then_inc(step, 1)
    dve.wait_ge(step, done + 1)
    dve.tensor_tensor(root[:, 2, :], out, out, ALU.mult).then_inc(step, 1)
    dve.wait_ge(step, done + 2)
    dve.tensor_tensor(root[:, 2, :], root[:, 2, :], root[:, 0, :], ALU.mult).then_inc(step, 1)
    dve.wait_ge(step, done + 3)
    dve.tensor_scalar(root[:, 2, :], root[:, 2, :], -0.5, 1.5, ALU.mult, ALU.add).then_inc(step, 1)
    dve.wait_ge(step, done + 4)
    dve.tensor_tensor(out, out, root[:, 2, :], ALU.mult).then_inc(step, 1)
    dve.wait_ge(step, done + 5)


def inverse_root(dve, var, eps, root, out, step, done, root_ready, roots, scale=1.0):
    root_input(dve, var, eps, root, step, done, scale)
    inverse_of_root(dve, root, out, step, done + 1, root_ready, roots)


def reached_apart(eng, sem, count, passed):
    if not (isinstance(count, int) and count <= 0):
        eng.wait_ge(sem, count)
        eng.sem_inc(passed, 1)


STEPS = KS + KC
LOAD_A = 16 * 12
LOAD_B = 16 * 12
Q_STACK = [0, 1, 2, 0, 1, 0]
K_STACK = [0, 0, 0, 1, 1, 2]

PAIR_OF_ONES = float(np.uint32(0x3F803F80).view(np.float32))


class Stacks:

    def __init__(self, ctx, nc, slot):
        def sb(name, shape, dt):
            return ctx.enter_context(nc.sbuf_tensor(f"{name}{slot}", shape, dt))

        self.q_self, self.k_self = sb("q_self", [P, GH, T], BF16), sb("k_self", [P, GH, T], BF16)
        self.q_cross, self.k_cross = sb("q_cross", [P, GH, T], BF16), sb("k_cross", [P, GH, TC], BF16)
        self.values = sb("values_in", [P, STEPS, GH * D], F32)
        self.self_loaded = ctx.enter_context(nc.semaphore(f"self_loaded{slot}"))
        self.cross_loaded = ctx.enter_context(nc.semaphore(f"cross_loaded{slot}"))
        self.values_loaded = ctx.enter_context(nc.semaphore(f"values_loaded{slot}"))

    def set_ones(self, eng, done, before):
        for i, t in enumerate((self.k_self, self.k_cross)):
            if before + i:
                eng.wait_ge(done, before + i)
            eng.memset(t[PAIR_ROWS:P].rearrange("p j t -> p (j t)").bitcast(F32), PAIR_OF_ONES).then_inc(done, 1)

    def load_self(self, sp, scr, n):
        for dst, name, parts in ((self.q_self, "q", Q_STACK), (self.k_self, "k", K_STACK)):
            load_stack(sp, dst, scr[name], n, parts, self.self_loaded)

    def load_cross(self, sp, scr, n):
        for dst, name, parts in ((self.q_cross, "qc", Q_STACK), (self.k_cross, "kc", K_STACK)):
            load_stack(sp, dst, scr[name], n, parts, self.cross_loaded)
        sp.dma_start(self.values[:, :, :], scr["v"].rearrange("b g p k f -> (b g) p k f")[n])\
          .then_inc(self.values_loaded, 16)


def load_stack(sp, dst, src, n, parts, loaded):
    rows = src.rearrange("b (g j) d p t -> (b g) p d j t", j=GH)
    for r, p in enumerate(parts):
        sp.dma_start(dst[r * D:(r + 1) * D], rows[n, p]).then_inc(loaded, 16)


LAST_CTX_JOB = ("split", "kc", 1, 1)
JOBS = [("split", "kc", 0, 0), ("turn", 0), ("value", KS + 0), ("turn", 1), ("split", "kc", 1, 0),
        ("split", "q", 0, 0), ("value", KS + 2), ("split", "kc", 0, 1), ("value", KS + 4),
        ("split", "q", 1, 0), ("value", KS + 6), LAST_CTX_JOB,
        ("split", "k", 0, 0), ("value", 0), ("split", "k", 1, 0),
        ("split", "qc", 0, 0), ("value", 2), ("split", "qc", 1, 0)]
MEASURE_JOB, ROOT_JOB, NORM_JOB = ("value", KS + 6), ("split", "k", 0, 0), ("split", "k", 1, 0)
CTX_SPLITS = sum(j[0] == "split" for j in JOBS[:JOBS.index(LAST_CTX_JOB) + 1])
NS = sum(j[0] == "split" for j in JOBS)
NV = sum(j[0] == "value" for j in JOBS)
LN_STEPS = 2 * QT + ROOT_STEPS
S_PSUM, V_PSUM, PARTS = 5, 2, 5
V_RUN = 2
V_RUNS = NV // V_RUN
assert NS % S_PSUM == 0 and NS % PARTS == 0 and NV % V_RUN == 0 and NS % 2 == 0 and NV % V_PSUM == 0


def build_projections(nc, a, scr, first_stacks, ones_set):
    with ExitStack() as ctx:
        def sb(name, shape, dt=F32):
            return ctx.enter_context(nc.sbuf_tensor(name, shape, dt))

        def sem(name):
            return ctx.enter_context(nc.semaphore(name))

        x_in = sb("x_in", [P, QT, C])
        ctx_in = sb("ctx_in", [P, TC])
        w_in = {n: sb(f"w_{n}", [P, CH, C]) for n in ("q", "k", "v", "qc")}
        wc_in = {n: sb(f"w_{n}", [P, C]) for n in ("kc", "vc")}
        b_col = {n: sb(f"b_{n}", [P, CH]) for n in ("q", "k", "qc", "kc")}
        b_row = {n: sb(f"b_{n}", [P, C]) for n in ("v", "vc")}
        ident = sb("ident_a", [P, P])
        stats = sb("stats_a", [P, QT, 6])
        mean_var = sb("mean_var_a", [P, QT, 2])
        rstd = sb("rstd_a", [P, QT])
        root = sb("root_a", [P, 3, QT])
        xn = sb("xn", [P, QT, C])
        xnT = sb("xnT", [P, CH, T])
        proj = sb("proj", [P, 2, T])
        rest = sb("rest", [P, 2, T])
        parts = sb("parts", [P, PARTS, NSPLIT, T], BF16)
        v_out = sb("v_out", [P, V_RUNS, H // GH, 2 * V_RUN, GH * D])
        ps_split = [ctx.enter_context(nc.psum_tensor(f"ps_split{i}", [P, T], F32)) for i in range(S_PSUM)]
        ps_value = [ctx.enter_context(nc.psum_tensor(f"ps_value{i}", [P, 2, C], F32)) for i in range(V_PSUM)]
        ps_xT = ctx.enter_context(nc.psum_tensor("ps_xT", [P, T], F32))

        wc_loaded = sem("wc_loaded")
        w_loaded, b_loaded, x_loaded, ctx_loaded = sem("w_loaded"), sem("b_loaded"), sem("x_loaded"), sem("ctx_loaded")
        ident_ready = sem("ident_a_ready")
        ln_step, root_ready, xn_ready = sem("ln_step_a"), sem("root_a_ready"), sem("xn_ready")
        xT_ready, xT_copied = sem("xT_ready"), sem("xT_copied")
        split_mm, part1 = sem("split_mm"), sem("part1")
        rest1, part2, part3 = sem("rest1"), sem("part2"), sem("part3")
        part_stored = [sem(f"part_stored{i}") for i in range(PARTS)]
        value_mm, value_copied = sem("value_mm"), sem("value_copied")
        value_stored = [sem(f"value_stored{i}") for i in range(V_RUNS)]
        N_BIASES = 6

        dve_passed, sp_passed = sem("dve_passed_a"), sem("sp_passed_a")
        block = ctx.enter_context(nc.Block())

        @block.sync
        def _(sp):
            def load_ctx(b):
                sp.dma_start(ctx_in[:, :], a["ctxT"][b]).then_inc(ctx_loaded, 16)

            def load_x(b):
                sp.dma_start(x_in[:, :, :], a["x"][b].rearrange("(j p) c -> p j c", p=P)).then_inc(x_loaded, 16)

            load_x(0)
            load_ctx(0)
            for n, src in (("kc", "Wck"), ("vc", "Wcv")):
                sp.dma_start(wc_in[n][:, :], a[src]).then_inc(wc_loaded, 16)
            for n, src in (("q", "Wq"), ("k", "Wk"), ("v", "Wv"), ("qc", "Wcq")):
                sp.dma_start(w_in[n][:, :, :], a[src].rearrange("(c p) n -> p c n", p=P)).then_inc(w_loaded, 16)

            def body(b, last):
                if not last:
                    sp.wait_ge(xn_ready, b + 1)
                    load_x(b + 1)
                s = v = 0
                for job in JOBS:
                    if job == LAST_CTX_JOB and not last:
                        sp.wait_ge(split_mm, b * NS + CTX_SPLITS)
                        load_ctx(b + 1)
                    if job[0] == "split":
                        _, dst, m, blk = job
                        reached_apart(sp, part3, b * NS + s + 1 + 2, sp_passed)
                        cols = slice(blk * T, (blk + 1) * T)
                        sp.dma_start(scr[dst][b, m * (P // D):(m + 1) * (P // D), :, :, cols].rearrange("h d p t -> (h d) p t"),
                                     parts[:, s % PARTS, :, :]).then_inc(part_stored[s % PARTS], 16)
                        s += 1
                    elif job[0] == "value":
                        v += 1
                        if v % V_RUN == 0:
                            reached_apart(sp, value_copied, b * NV + v + V_PSUM, sp_passed)
                            tiles = slice(job[1] + 2 - 2 * V_RUN, job[1] + 2)
                            sp.dma_start(scr["v"][b, :, :, tiles, :].rearrange("g p k f -> p g (k f)"),
                                         v_out[:, v // V_RUN - 1].rearrange("p g k f -> p g (k f)"))\
                              .then_inc(value_stored[v // V_RUN - 1], 16)

            with sp.Fori(0, B - 1) as b:
                body(b, False)
            for i in range(PARTS):
                sp.wait_ge(part_stored[i], 16 * (NS // PARTS + 1))
            for i in range(V_RUNS):
                sp.wait_ge(value_stored[i], 16 * (1 + 1))
            first_stacks.load_self(sp, scr, 0)
            first_stacks.load_cross(sp, scr, 0)
            body(B - 1, True)
            for i in range(PARTS):
                sp.wait_ge(part_stored[i], 16 * (B * (NS // PARTS) + 1))
            for i in range(V_RUNS):
                sp.wait_ge(value_stored[i], 16 * (B + 1))

        @block.gpsimd
        def _(pool):
            for q in part_stored:
                pool.sem_inc(q, 16)
            for n, src in (("q", "bq"), ("k", "bk"), ("qc", "bcq"), ("kc", "bck")):
                pool.dma_start(b_col[n][:, :], a[src]).then_inc(b_loaded, 16)
            for n, src in (("v", "bv"), ("vc", "bcv")):
                pool.dma_start(b_row[n][:, :], a[src].rearrange("(o n) -> o n", o=1).to_broadcast([P, C]))\
                    .then_inc(b_loaded, 16)
            pool.memset(ident[:, :], 0.0).then_inc(ident_ready, 1)
            pool.wait_ge(ident_ready, 1)
            pool.affine_select(out=ident[:, :], in_=ident[:, :], compare_op=ALU.not_equal, fill=1.0,
                               base=0, pattern=[[-1, P]], channel_multiplier=1).then_inc(ident_ready, 1)
            pool.wait_ge(ident_ready, 2)
            first_stacks.set_ones(pool, ones_set, 0)

        @block.scalar
        def _(act):
            act.sem_inc(part1, S_PSUM)
            act.sem_inc(xT_copied, 1)

            def take_root(b):
                act.wait_ge(ln_step, b * LN_STEPS + 2 * QT + 1)
                act.activation(root[:, 1, :], root[:, 0, :], ACT.Sqrt).then_inc(root_ready, 1)

            def body(b, last):
                def second_part(s):
                    act.wait_ge(rest1, b * NS + s + 1 + 2)
                    act.activation(parts[:, s % PARTS, 1, :], rest[:, s % 2, :], ACT.Identity).then_inc(part2, 1)

                s = 0
                for job in JOBS:
                    if job[0] == "turn":
                        c = job[1]
                        act.wait_ge(xT_ready, b * CH + c + 1 + CH)
                        act.activation(xnT[:, c, :], ps_xT[:, :], ACT.Identity).then_inc(xT_copied, 1)
                    if job[0] != "split":
                        continue
                    bias = b_col[job[1]][:, job[2]:job[2] + 1]
                    act.wait_ge(split_mm, b * NS + s + 1)
                    act.wait_ge(rest1, b * NS + s + 1)
                    act.activation(proj[:, s % 2, :], ps_split[s % S_PSUM][:, :], ACT.Identity, bias=bias)
                    act.wait_ge(part_stored[s % PARTS], (b * (NS // PARTS) + s // PARTS + 1) * 16)
                    act.activation(parts[:, s % PARTS, 0, :], ps_split[s % S_PSUM][:, :], ACT.Identity, bias=bias)\
                       .then_inc(part1, 1)
                    if s:
                        second_part(s - 1)
                    if job == ROOT_JOB and not last:
                        take_root(b + 1)
                    s += 1
                second_part(NS - 1)

            take_root(0)
            act.wait_ge(b_loaded, 16 * N_BIASES)
            with act.Fori(0, B - 1) as b:
                body(b, False)
            body(B - 1, True)

        @block.vector
        def _(dve):
            dve.sem_inc(rest1, 2)
            dve.sem_inc(part3, 2)
            dve.sem_inc(value_copied, V_PSUM)
            for q in value_stored:
                dve.sem_inc(q, 16)

            def measure(b):
                reached_apart(dve, x_loaded, (b + 1) * 16, dve_passed)
                for j in range(QT):
                    dve.bn_stats(stats[:, j, :], x_in[:, j, :]).then_inc(ln_step, 1)
                for j in range(QT):
                    reached_apart(dve, ln_step, b * LN_STEPS + j + 1, dve_passed)
                    dve.bn_aggr(mean_var[:, j, :], stats[:, j, :]).then_inc(ln_step, 1)
                root_input(dve, mean_var[:, :, 1], LN_EPS, root, ln_step, b * LN_STEPS + 2 * QT)

            def norm(b):
                inverse_of_root(dve, root, rstd[:, :], ln_step, b * LN_STEPS + 2 * QT + 1, root_ready, b + 1)
                dve.wait_ge(xT_ready, b * CH + CH)
                for j in range(QT):
                    ins = dve.tensor_scalar(xn[:, j, :], x_in[:, j, :], mean_var[:, j, 0:1], rstd[:, j:j + 1],
                                            ALU.subtract, ALU.mult)
                ins.then_inc(xn_ready, 1)

            def body(b, last):
                def third_part(s):
                    dve.wait_ge(part2, b * NS + s + 1)
                    dve.tensor_tensor(parts[:, s % PARTS, 2, :], rest[:, s % 2, :], parts[:, s % PARTS, 1, :],
                                      ALU.subtract).then_inc(part3, 1)

                s = v = 0
                for job in JOBS:
                    if job[0] == "split":
                        dve.wait_ge(part1, b * NS + s + 1 + S_PSUM)
                        dve.wait_ge(part3, b * NS + s + 1)
                        dve.tensor_tensor(rest[:, s % 2, :], proj[:, s % 2, :], parts[:, s % PARTS, 0, :],
                                          ALU.subtract).then_inc(rest1, 1)
                        if s:
                            third_part(s - 1)
                        s += 1
                    elif job[0] == "value":
                        dve.wait_ge(value_mm, b * NV + v + 1)
                        dve.wait_ge(value_stored[v // V_RUN], b * 16 + 16)
                        bias = b_row["v" if job[1] < KS else "vc"]
                        at = v % V_RUN * 2
                        dve.tensor_tensor(v_out[:, v // V_RUN, :, at:at + 2, :].rearrange("p g k f -> p k g f"),
                                          ps_value[v % V_PSUM][:, :, :].rearrange("p k (g f) -> p k g f", g=H // GH),
                                          bias[:, :].rearrange("p (o g f) -> p o g f", o=1, g=H // GH)
                                          .to_broadcast([P, 2, H // GH, GH * D]), ALU.add)\
                           .then_inc(value_copied, 1)
                        v += 1
                    if job == MEASURE_JOB and not last:
                        measure(b + 1)
                    if job == NORM_JOB and not last:
                        norm(b + 1)
                third_part(NS - 1)

            measure(0)
            norm(0)
            dve.wait_ge(b_loaded, 16 * N_BIASES)
            with dve.Fori(0, B - 1) as b:
                body(b, False)
            body(B - 1, True)

        @block.tensor
        def _(pe):
            pe.sem_inc(xT_ready, CH)
            pe.wait_ge(ident_ready, 2)
            pe.wait_ge(wc_loaded, 16 * len(wc_in))
            with pe.Fori(0, B) as b:
                pe.wait_ge(ctx_loaded, (b + 1) * 16)
                s = v = 0
                for job in JOBS:
                    if job[0] == "turn":
                        c = job[1]
                        if c == 0:
                            pe.wait_ge(xn_ready, b + 1)
                        pe.wait_ge(xT_copied, b * CH + c + 1)
                        for j in range(QT):
                            ins = pe.transpose(ps_xT[:, j * P:(j + 1) * P], xn[:, j, c * P:(c + 1) * P], ident[:, :])
                        ins.then_inc(xT_ready, 1)
                    if job[0] == "split":
                        _, name, m, blk = job
                        pe.wait_ge(part1, b * NS + s + 1)
                        out = ps_split[s % S_PSUM][:, :]
                        if name == "q" and m == 0:
                            pe.wait_ge(w_loaded, 16 * len(w_in))
                            pe.wait_ge(xT_copied, b * CH + CH + 1)
                        if name == "kc":
                            ins = pe.matmul(out, wc_in["kc"][:, m * P:(m + 1) * P], ctx_in[:, blk * T:(blk + 1) * T],
                                            start=True, stop=True)
                        else:
                            for c in range(CH):
                                ins = pe.matmul(out, w_in[name][:, c, m * P:(m + 1) * P], xnT[:, c, :],
                                                start=(c == 0), stop=(c == CH - 1))
                        ins.then_inc(split_mm, 1)
                        s += 1
                    elif job[0] == "value":
                        pe.wait_ge(value_copied, b * NV + v + 1)
                        for j in (job[1], job[1] + 1):
                            out = ps_value[v % V_PSUM][:, j % 2, :]
                            if j >= KS:
                                ins = pe.matmul(out, ctx_in[:, (j - KS) * P:(j - KS + 1) * P], wc_in["vc"][:, :],
                                                start=True, stop=True)
                            else:
                                for c in range(CH):
                                    ins = pe.matmul(out, xnT[:, c, j * P:(j + 1) * P], w_in["v"][:, c, :],
                                                    start=(c == 0), stop=(c == CH - 1))
                        ins.then_inc(value_mm, 1)
                        v += 1


UNITS = 2 * GH * QT
SELF_UNITS = GH * QT
MAX_BANKS = 4
assert E == (NG - 2) // 2 + 1
ROWS = NSPLIT * GH * QT


BANKS = 3
BANK_JOBS = []
for _step in range(STEPS):
    BANK_JOBS += [("score", _step * GH + h) for h in range(GH)]
    BANK_JOBS += {0: [("rows", 1)], 1: [("sums", 1)], KS + 2: [("sums", 0)], KS + 4: [("rows", 0)]}.get(_step, [])
assert len(BANK_JOBS) % BANKS == 1
BANK_OF = {job: i % BANKS for i, job in enumerate(BANK_JOBS)}
BANK_OF[BANK_JOBS[-1]] = 1


def units_of_step(k):
    if k < KS:
        return range(GH * k, GH * k + GH)
    return range(SELF_UNITS + 2 * (k - KS), SELF_UNITS + 2 * (k - KS) + 2)


def build_attention(nc, scr, first_stacks, ones_set, y_all, experts):
    with ExitStack() as ctx:
        def sb(name, shape, dt=F32):
            return ctx.enter_context(nc.sbuf_tensor(name, shape, dt))

        def sem(name):
            return ctx.enter_context(nc.semaphore(name))

        stacks = [first_stacks, Stacks(ctx, nc, 1)]
        q_self, k_self = [t.q_self for t in stacks], [t.k_self for t in stacks]
        q_cross, k_cross = [t.q_cross for t in stacks], [t.k_cross for t in stacks]
        self_loaded, cross_loaded = [t.self_loaded for t in stacks], [t.cross_loaded for t in stacks]
        values = [sb(f"values{i}", [P, STEPS, GH * VW]) for i in range(2)]
        ident = sb("ident_b", [P, P])
        ident_h = sb("ident_bh", [P, P], BF16)
        mask_q = sb("mask_q", [P, P], BF16)
        neg_max = [sb(f"neg_max{i}", [P, GH * QT]) for i in range(2)]
        neg_rest = [sb(f"neg_rest{i}", [P, GH * QT]) for i in range(2)]
        neg_parts = [sb(f"neg_parts{i}", [P, NSPLIT, GH * QT], BF16) for i in range(2)]
        shift_rows = [sb(f"shift_rows{i}", [ROWS, P], BF16) for i in range(2)]
        probs = [sb(f"probs{i}", [P, GH, T]) for i in range(2)]
        sums = [sb(f"sums{i}", [P, T]) for i in range(2)]
        inv = [sb(f"inv{i}", [P, GH * QT]) for i in range(2)]
        y_cross = sb("y_cross", [P, QT, GH, D])
        ps_max = [ctx.enter_context(nc.psum_tensor(f"ps_max{i}", [P, TC], F32)) for i in range(2)]
        ps_bank = [ctx.enter_context(nc.psum_tensor(f"ps_bank{i}", [P, T], F32)) for i in range(BANKS)]
        ps_sum = ctx.enter_context(nc.psum_tensor("ps_sum", [P, T], F32))

        def bank(job):
            return ps_bank[BANK_OF[job]]

        def rows_bank(kind):
            return bank(("rows", kind))[:, :].bitcast(BF16)[0:ROWS, 0:P]

        def max_bank(u):
            return ps_max[u % MAX_BANKS // 2][:, u % 2 * T:(u % 2 + 1) * T]

        consts = sem("consts_b")
        shift_self = [sem(f"shift_self{i}") for i in range(2)]
        shift_cross = [sem(f"shift_cross{i}") for i in range(2)]
        pads_set, values_ready = sem("pads_set"), sem("values_ready")
        masked = sem("masked")
        scores_ready, probs_ready, summed = sem("scores_ready"), sem("probs_ready"), sem("summed")
        unit_ready, unit_max = sem("unit_ready"), sem("unit_max")
        split_step, neg_split = sem("split_step"), sem("neg_split")
        rows_turned, sums_turned = sem("rows_turned"), sem("sums_turned")
        rows_copied, sums_copied = sem("rows_copied"), sem("sums_copied")
        inv_ready, scaled, y_added = sem("inv_ready"), sem("scaled"), sem("y_added")

        pe_passed, pool_passed, sp_passed = sem("pe_passed_b"), sem("pool_passed_b"), sem("sp_passed_b")
        block = ctx.enter_context(nc.Block())

        def groups(eng, group):
            group(0, 0, 1, False, True)
            with eng.Fori(0, (NG - 2) // 2) as i:
                group(i * 2 + 1, 1, i + 1, True, True)
                group(i * 2 + 2, 0, i + 2, True, True)
            group(NG - 1, 1, NG // 2, True, False)

        @block.sync
        def _(sp):
            stacks[1].load_self(sp, scr, 1)
            stacks[1].load_cross(sp, scr, 1)
            a, w_gate, w_down, experts_loaded = experts

            def load_weights(e, which):
                w, name = ((w_gate, "gating_w"), (w_down, "linear_w"))[which]
                m = w.shape[1] // E
                sp.dma_start(w[:, bass.ds(e * m, m)], a[name][:, bass.ds(e * m, m)]).then_inc(experts_loaded, 16)

            with sp.Fori(0, (NG - 2) // 2) as i:
                for s in range(2):
                    n = i * 2 + s
                    reached_apart(sp, scores_ready, (n * STEPS + KS) * GH, sp_passed)
                    stacks[s].load_self(sp, scr, n + 2)
                    reached_apart(sp, scores_ready, (n * STEPS + STEPS) * GH, sp_passed)
                    stacks[s].load_cross(sp, scr, n + 2)
                    load_weights(i, s)
            for which in range(2):
                load_weights(E - 1, which)

        @block.gpsimd
        def _(pool):
            pool.memset(ident[:, :], 0.0).then_inc(split_step, 1)
            pool.memset(ident_h[:, :], 0.0).then_inc(split_step, 1)
            pool.memset(mask_q[:, :], 0.0).then_inc(split_step, 1)
            pool.wait_ge(split_step, 3)
            for t in (ident, ident_h):
                pool.affine_select(out=t[:, :], in_=t[:, :], compare_op=ALU.not_equal, fill=1.0,
                                   base=0, pattern=[[-1, P]], channel_multiplier=1).then_inc(consts, 1)
            pool.affine_select(out=mask_q[:, :], in_=mask_q[:, :], compare_op=ALU.is_ge, fill=MASKED,
                               base=0, pattern=[[-1, P]], channel_multiplier=1).then_inc(consts, 1)

            def split_maxima(kind, n):
                at = (n * 2 + kind) * 3 + 3
                nm, rest, parts = neg_max[kind], neg_rest[kind], neg_parts[kind]
                reached_apart(pool, unit_max, n * UNITS + SELF_UNITS * (kind + 1), pool_passed)
                pool.tensor_copy(parts[:, 0, :], nm[:, :]).then_inc(split_step, 1)
                pool.wait_ge(split_step, at + 1)
                pool.tensor_tensor(rest[:, :], nm[:, :], parts[:, 0, :], ALU.subtract).then_inc(split_step, 1)
                reached_apart(pool, split_step, at + 2, pool_passed)
                pool.tensor_copy(parts[:, 1, :], rest[:, :]).then_inc(split_step, 1)
                pool.wait_ge(split_step, at + 3)
                pool.tensor_tensor(parts[:, 2, :], rest[:, :], parts[:, 1, :], ALU.subtract).then_inc(neg_split, 1)

            def send_rows(kind, n, slot):
                stack = (q_self, q_cross)[kind][slot]
                reached_apart(pool, rows_copied, n * 2 + kind + 1, pool_passed)
                pool.dma_start(stack[PAIR_ROWS:PAIR_ROWS + SHIFT_ROWS].rearrange("p j t -> p (j t)"),
                               shift_rows[kind][:, :]).then_inc((shift_self, shift_cross)[kind][slot], 16)

            def place_values(n, slot, k):
                reached_apart(pool, stacks[slot].values_loaded, k * 16, pool_passed)
                reached_apart(pool, summed, n * STEPS - STEPS, pool_passed)
                pool.tensor_copy(values[slot][:, :, :].rearrange("p k (j f) -> p (k j) f", j=GH)[:, :, 1:1 + D],
                                 stacks[slot].values[:, :, :].rearrange("p k (j f) -> p (k j) f", j=GH))\
                    .then_inc(values_ready, 1)

            def mask_probs(n, step):
                for h in range(0, GH, 2):
                    at = (n * KS + step) * GH + h
                    reached_apart(pool, masked, at, pool_passed)
                    reached_apart(pool, probs_ready, (n * STEPS + step) * GH + h + 2, pool_passed)
                    tiles = probs[step % 2][:, h:h + 2, step * P:(step + 1) * P]
                    pool.affine_select(out=tiles, in_=tiles, compare_op=ALU.is_ge, fill=0.0, base=0,
                                       pattern=[[0, 2], [1, P]], channel_multiplier=-1).then_inc(masked, 2)

            def add_cross(n):
                reached_apart(pool, scaled, n * 2 + 2, pool_passed)
                y = y_all[:, n, :, :]
                pool.tensor_tensor(y, y, y_cross[:, :, :, :].rearrange("p q j d -> p q (j d)"), ALU.add)\
                    .then_inc(y_added, 1)

            def group(n, slot, k, prev, nxt):
                reached_apart(pool, neg_split, n * 2 + 2, pool_passed)
                mask_probs(n, 0)
                send_rows(1, n, slot)
                mask_probs(n, 1)
                mask_probs(n, 2)
                mask_probs(n, 3)
                reached_apart(pool, masked, (n + 1) * KS * GH, pool_passed)
                if prev:
                    add_cross(n - 1)
                    reached_apart(pool, y_added, n, pool_passed)
                if nxt:
                    split_maxima(0, n + 1)
                    send_rows(0, n + 1, 1 - slot)
                    place_values(n + 1, 1 - slot, k + (slot == 1))
                    split_maxima(1, n + 1)

            for v in values:
                pool.memset(v[:, :, :], 0.0).then_inc(pads_set, 1)
            pool.wait_ge(pads_set, 2)
            for v in values:
                pool.memset(v[:, :, :].rearrange("p k (j f) -> p (k j) f", j=GH)[:, :, 0:1], 1.0).then_inc(pads_set, 1)
            pool.wait_ge(pads_set, 4)
            split_maxima(0, 0)
            send_rows(0, 0, 0)
            place_values(0, 0, 1)
            pool.wait_ge(values_ready, 1)
            stacks[1].set_ones(pool, ones_set, 2)
            pool.wait_ge(ones_set, 4)
            split_maxima(1, 0)
            groups(pool, group)
            add_cross(NG - 1)

        @block.scalar
        def _(act):
            def copy_rows(kind, n):
                act.wait_ge(rows_turned, n * 2 + kind + 1)
                act.activation(shift_rows[kind][:, :], rows_bank(kind), ACT.Copy).then_inc(rows_copied, 1)

            def copy_sums(kind, n):
                act.wait_ge(summed, n * STEPS + (STEPS if kind else KS))
                act.activation(sums[kind][:, :], ps_sum[:, :], ACT.Copy).then_inc(sums_copied, 1)

            def group(n, slot, k, prev, nxt):
                for step in range(STEPS):
                    off = step * P if step < KS else 0
                    reached(act, summed, n * STEPS + step - 1)
                    for h in range(GH):
                        g = (n * STEPS + step) * GH + h
                        act.wait_ge(scores_ready, g + 1)
                        act.activation(probs[step % 2][:, h, off:T], bank(("score", step * GH + h))[:, off:T], ACT.Exp,
                                       scale=SCALE)\
                           .then_inc(probs_ready, 1)
                    if step == 0:
                        copy_rows(1, n)
                        if prev:
                            copy_sums(1, n - 1)
                    if step == KS:
                        copy_sums(0, n)
                    if step == KS + 4 and nxt:
                        copy_rows(0, n + 1)

            copy_rows(0, 0)
            groups(act, group)
            copy_sums(1, NG - 1)

        @block.vector
        def _(dve):
            def units(n, us):
                for u in us:
                    h, t = divmod(u % SELF_UNITS, QT)
                    kind = u // SELF_UNITS
                    scores = ps_max[u % 2][:, :] if kind else max_bank(u)[:, 0:(t + 1) * P]
                    dve.wait_ge(unit_ready, n * UNITS + u + 1)
                    dve.tensor_reduce(neg_max[kind][:, h * QT + t:h * QT + t + 1], scores,
                                      AX.X, ALU.max, negate=True).then_inc(unit_max, 1)

            def normalise(kind, n):
                t = bank(("sums", kind))[:, :].rearrange("p (q j f) -> p q j f", q=QT, j=GH)
                v = inv[kind][:, :].rearrange("p (q j f) -> p q j f", q=QT, j=GH)
                dve.wait_ge(sums_turned, n * 2 + kind + 1)
                dve.reciprocal(v, t[:, :, :, 0:1]).then_inc(inv_ready, 1)
                dve.wait_ge(inv_ready, n * 2 + kind + 1)
                if kind:
                    reached(dve, y_added, n)
                    out = y_cross[:, :, :, :]
                else:
                    out = y_all[:, n, :, :].rearrange("p q (j d) -> p q j d", j=GH)
                dve.tensor_tensor(out, t[:, :, :, 1:1 + D], v.to_broadcast([P, QT, GH, D]), ALU.mult)\
                   .then_inc(scaled, 1)

            def group(n, slot, k, prev, nxt):
                for step in range(STEPS):
                    if nxt:
                        units(n + 1, units_of_step(step))
                    if step == 1 and prev:
                        normalise(1, n - 1)
                    if step == KS + 2:
                        normalise(0, n)

            units(0, range(UNITS))
            groups(dve, group)
            normalise(1, NG - 1)

        @block.tensor
        def _(pe):
            def unit(n, u, slot):
                h, t = divmod(u % SELF_UNITS, QT)
                q = (q_self, q_cross)[u // SELF_UNITS][slot][0:PAIR_ROWS, h, t * P:(t + 1) * P]
                if u < SELF_UNITS:
                    reached(pe, unit_max, n * UNITS + (u - 3 if u >= MAX_BANKS else u // 2 - 1))
                    out = max_bank(u)
                    pe.matmul(out[:, 0:(t + 1) * P], q, k_self[slot][0:PAIR_ROWS, h, 0:(t + 1) * P],
                              start=True, stop=False)
                    pe.matmul(out[:, t * P:(t + 1) * P], ident_h[:, :], mask_q[:, :],
                              start=False, stop=True).then_inc(unit_ready, 1)
                    return
                before = u - SELF_UNITS
                reached(pe, unit_max, n * UNITS + (u - 1 if before >= 2 else SELF_UNITS - 2 + 2 * before))
                for c in range(TC // T):
                    ins = pe.matmul(ps_max[u % 2][:, c * T:(c + 1) * T], q,
                                    k_cross[slot][0:PAIR_ROWS, h, c * T:(c + 1) * T], start=True, stop=True)
                ins.then_inc(unit_ready, 1)

            def take_bank(job, n):
                at = BANK_JOBS.index(job)
                back = next(d for d in range(1, len(BANK_JOBS)) if BANK_OF[BANK_JOBS[at - d]] == BANK_OF[job])
                kind, which = BANK_JOBS[at - back]
                m = n if back <= at else n - 1
                if kind == "score":
                    reached(pe, probs_ready, m * STEPS * GH + which + 1)
                elif kind == "rows":
                    if which or not (isinstance(m, int) and m == NG - 1):
                        reached(pe, rows_copied, m * 2 + (2 if which else 3))
                else:
                    reached(pe, scaled, m * 2 + (0 if which else 1))
                return bank(job)

            def scores(n, step, h, slot):
                last = PAIR_ROWS + SHIFT_ROWS
                out = take_bank(("score", step * GH + h), n)
                if step < KS:
                    off = step * P
                    ins = pe.matmul(out[:, off:T], k_self[slot][0:last, h, off:off + P], q_self[slot][0:last, h, off:T],
                                    start=True, stop=True)
                else:
                    off = (step - KS) * P
                    ins = pe.matmul(out[:, :], k_cross[slot][0:last, h, off:off + P], q_cross[slot][0:last, h, :],
                                    start=True, stop=True)
                ins.then_inc(scores_ready, 1)

            def weigh(n, step, slot):
                off = step * P if step < KS else 0
                first = step in (0, KS)
                last = step in (KS - 1, STEPS - 1)
                if first:
                    reached(pe, sums_copied, n * 2 + (1 if step else 0))
                if step < KS:
                    pe.wait_ge(masked, (n * KS + step + 1) * GH)
                else:
                    pe.wait_ge(probs_ready, (n * STEPS + step + 1) * GH)
                for h in range(GH):
                    ins = pe.matmul(ps_sum[h * VW:(h + 1) * VW, off:T], values[slot][:, step, h * VW:(h + 1) * VW],
                                    probs[step % 2][:, h, off:T], start=first, stop=last, tile_position=(0, h * VW))
                ins.then_inc(summed, 1)

            def turn_rows(kind, n):
                if not (isinstance(n, int) and n + kind == 0):
                    take_bank(("rows", kind), n if kind else n - 1)
                reached_apart(pe, neg_split, n * 2 + kind + 1, pe_passed)
                pe.transpose(rows_bank(kind), neg_parts[kind][:, :, :].rearrange("p s j -> p (s j)"),
                             ident_h[:, :]).then_inc(rows_turned, 1)

            def turn_sums(kind, n):
                if kind and isinstance(n, int) and n == NG - 1:
                    out = bank(("sums", kind))
                else:
                    out = take_bank(("sums", kind), n + 1 if kind else n)
                pe.wait_ge(sums_copied, n * 2 + kind + 1)
                for t in range(QT):
                    ins = pe.transpose(out[:, t * P:(t + 1) * P], sums[kind][:, t * P:(t + 1) * P], ident[:, :])
                ins.then_inc(sums_turned, 1)

            def group(n, slot, k, prev, nxt):
                for step in range(STEPS):
                    if step == 0:
                        pe.wait_ge(shift_self[slot], k * 16)
                        if nxt:
                            pe.wait_ge(self_loaded[1 - slot], (k + (slot == 1)) * LOAD_A)
                    if step == 1:
                        pe.wait_ge(values_ready, n + 1)
                    if step == KS:
                        pe.wait_ge(shift_cross[slot], k * 16)
                        if nxt:
                            pe.wait_ge(cross_loaded[1 - slot], (k + (slot == 1)) * LOAD_B)
                    if not nxt:
                        fill = ((), (), (), ())
                    elif step < KS:
                        fill = tuple((u,) for u in units_of_step(step))
                    else:
                        u0, u1 = units_of_step(step)
                        fill = ((u0,), (), (u1,), ())
                    for h in range(GH):
                        scores(n, step, h, slot)
                        for u in fill[h]:
                            unit(n + 1, u, 1 - slot)
                        if step and h == (GH - 1 if step <= KS else 1):
                            weigh(n, step - 1, slot)
                        elif not step and h == 1 and prev:
                            weigh(n - 1, STEPS - 1, 1 - slot)
                    if step == 0:
                        turn_rows(1, n)
                    elif step == KS + 4 and nxt:
                        turn_rows(0, n + 1)
                    if step == 1 and prev:
                        turn_sums(1, n - 1)
                    if step == KS + 2:
                        turn_sums(0, n)
                if not prev:
                    pe.wait_ge(ones_set, 4)

            pe.wait_ge(consts, 3)
            pe.wait_ge(self_loaded[0], LOAD_A)
            for u in range(SELF_UNITS):
                unit(0, u, 0)
            turn_rows(0, 0)
            pe.wait_ge(cross_loaded[0], LOAD_B)
            for u in range(SELF_UNITS, UNITS):
                unit(0, u, 0)
            pe.wait_ge(ones_set, 2)
            groups(pe, group)
            weigh(NG - 1, STEPS - 1, (NG - 1) % 2)
            turn_sums(1, NG - 1)


 
TOPK = 2
HID = 512
HC = HID // P
NT = B * T // P
SLOT_TILES = NT * TOPK + E - 1
DUMP = B * T


def build_router_inputs(nc, a, y_all, x2_rows, out_rows, logits):
    with ExitStack() as ctx:
        def sb(name, shape, dt=F32):
            return ctx.enter_context(nc.sbuf_tensor(name, shape, dt))

        def sem(name):
            return ctx.enter_context(nc.semaphore(name))

        wp = sb("wp", [P, CH, C])
        wr = sb("wr", [P, CH, E])
        wr_scaled = sb("wr_scaled", [P, CH, E])
        router_scale = sb("router_scale", [P, CH])
        bp_row = sb("bp_row", [P, C])
        zero_rows = sb("zero_rows", [P, C])
        ident = sb("ident_c", [P, P])
        x1 = sb("x1", [P, NT, C])
        y_in = [sb(f"y_in{i}", [P, QT, C]) for i in range(2)]
        x2 = [sb(f"x2_{i}", [P, QT, C]) for i in range(2)]
        turned = [sb(f"turned{i}", [P, CH, T]) for i in range(2)]
        squares = sb("squares", [P, C])
        stats = sb("stats_c", [P, QT, 6])
        mean_var = sb("mean_var_c", [P, NT, 2])
        square_sum = sb("square_sum", [P, NT])
        rstd = sb("rstd_c", [P, NT])
        rms = sb("rms_c", [P, NT])
        rms_scaled = sb("rms_scaled", [P, NT])
        root = sb("root_c", [P, 3, NT])
        ps_T = [ctx.enter_context(nc.psum_tensor(f"ps_T{i}", [P, T], F32)) for i in range(CH)]
        ps_o = [[ctx.enter_context(nc.psum_tensor(f"ps_proj{s}{i}", [P, 2, C], F32)) for i in range(QT // 2)]
                for s in range(2)]
        ps_l = ctx.enter_context(nc.psum_tensor("ps_logits", [P, NT, E], F32))

        loaded, bias_loaded, consts, wr_ready = sem("loaded_c"), sem("bias_loaded"), sem("consts_c"), sem("wr_ready")
        x_loaded = [sem(f"x_loaded_c{i}") for i in range(2)]
        y_copied, T_ready, T_copied = sem("y_copied"), sem("T_ready"), sem("T_copied")
        products, x_biased, x1_ready = sem("products_c"), sem("x_biased"), sem("x1_ready")
        ln_step, root_ready, x2_ready = sem("ln_step_c"), sem("root_c_ready"), sem("x2_ready")
        squared, logits_ready = sem("squared"), sem("logits_ready")
        x1_stored, spare_stored = sem("x1_stored"), sem("spare_stored")
        x2_stored = [sem(f"x2_stored{i}") for i in range(2)]
        N_LOADS = 3
        ROWS_STEPS = 2 * QT

        sp_passed = sem("sp_passed_c")
        block = ctx.enter_context(nc.Block())

        def batches(eng, body):
            with eng.Fori(0, B // 2) as i:
                for s in range(2):
                    body(i * 2 + s, s, i + 1)

        @block.sync
        def _(sp):
            for b in range(B):
                reached(sp, x_loaded[b % 2], b // 2 * 16)
                sp.dma_start(x1[:, b * QT:(b + 1) * QT, :], a["x"][b].rearrange("(j p) c -> p j c", p=P))\
                  .then_inc(x_loaded[b % 2], 16)
                if b == 0:
                    sp.dma_start(bp_row[:, :], a["bp"].rearrange("(o n) -> o n", o=1).to_broadcast([P, C]))\
                      .then_inc(bias_loaded, 16)
                    sp.dma_start(wp[:, :, :], a["Wp"].rearrange("(c p) n -> p c n", p=P)).then_inc(loaded, 16)
                    sp.dma_start(wr[:, :, :], a["router_w"].rearrange("(c p) e -> p c e", p=P)).then_inc(loaded, 16)
                    sp.dma_start(router_scale[:, :], a["router_scale"]).then_inc(loaded, 16)
            sp.wait_ge(consts, 3)
            for rows in (x2_rows, out_rows):
                sp.dma_start(rows[DUMP:DUMP + P], zero_rows[:, :]).then_inc(spare_stored, 16)

            def store_x1(b, s, k):
                reached_apart(sp, x1_ready, b + 1 + 2, sp_passed)
                sp.dma_start(out_rows[bass.ds(b * T, T)].rearrange("(j p) c -> p j c", p=P),
                             x1[:, bass.ds(b * QT, QT), :]).then_inc(x1_stored, 16)

            def store_x2(b, s, k):
                reached_apart(sp, x2_ready, b + 1, sp_passed)
                sp.dma_start(x2_rows[bass.ds(b * T, T)].rearrange("(j p) c -> p j c", p=P), x2[s][:, :, :])\
                  .then_inc(x2_stored[s], 16)

            batches(sp, store_x1)
            batches(sp, store_x2)
            sp.wait_ge(spare_stored, 16 * 2)
            sp.wait_ge(x1_stored, 16 * B)
            for s in range(2):
                sp.wait_ge(x2_stored[s], 16 * (B // 2 + 1))

        @block.gpsimd
        def _(pool):
            pool.memset(ident[:, :], 0.0).then_inc(consts, 1)
            pool.memset(zero_rows[:, :], 0.0).then_inc(consts, 1)
            pool.wait_ge(consts, 2)
            pool.affine_select(out=ident[:, :], in_=ident[:, :], compare_op=ALU.not_equal, fill=1.0,
                               base=0, pattern=[[-1, P]], channel_multiplier=1).then_inc(consts, 1)

            pool.wait_ge(bias_loaded, 16)

            def add_bias(b, s, k):
                pool.wait_ge(x_loaded[s], k * 16)
                rows = x1[:, bass.ds(b * QT, QT), :]
                pool.tensor_tensor(rows, rows, bp_row[:, :].rearrange("p (o c) -> p o c", o=1).to_broadcast([P, QT, C]),
                                   ALU.add).then_inc(x_biased, 1)

            batches(pool, add_bias)

        @block.scalar
        def _(act):
            act.sem_inc(T_copied, CH)

            def copy_turned(n, s, k):
                for c in range(CH):
                    act.wait_ge(T_ready, n * CH + c + 1 + 2 * CH)
                    act.wait_ge(products, 2 * n + 2)
                    act.activation(turned[s][:, c, :], ps_T[c][:, :], ACT.Identity).then_inc(T_copied, 1)

            with act.Fori(0, B // 2) as i:
                for s in range(2):
                    b = i * 2 + s
                    act.wait_ge(T_ready, b * CH + CH)
                    act.activation(y_in[s][:, :, :].rearrange("p q (g f) -> p g q f", g=H // GH),
                                   y_all[:, bass.ds(b * (H // GH), H // GH), :, :], ACT.Identity).then_inc(y_copied, 1)
                for s in range(2):
                    copy_turned(i * 2 + s, s, i + 1)
            act.wait_ge(ln_step, B * ROWS_STEPS + 1)
            act.activation(root[:, 1, :], root[:, 0, :], ACT.Sqrt).then_inc(root_ready, 1)
            batches(act, lambda b, s, k: copy_turned(b + B, s, k))
            act.wait_ge(ln_step, B * ROWS_STEPS + ROOT_STEPS + 1)
            act.activation(root[:, 1, :], root[:, 0, :], ACT.Sqrt).then_inc(root_ready, 1)

        @block.vector
        def _(dve):
            for q in x2_stored:
                dve.sem_inc(q, 16)
            dve.sem_inc(x1_ready, 2)
            dve.sem_inc(squared, 1)
            dve.wait_ge(loaded, 16 * N_LOADS)
            for c in range(CH):
                dve.tensor_scalar(wr_scaled[:, c, :], wr[:, c, :], router_scale[:, c:c + 1], None, ALU.mult)\
                   .then_inc(wr_ready, 1)

            def add_and_measure(b, s, k):
                dve.wait_ge(x_biased, b + 1)
                for i in range(QT // 2):
                    dve.wait_ge(products, 2 * b + i + 1 + 4)
                    rows = x1[:, b * QT + 2 * i:b * QT + 2 * i + 2, :]
                    ins = dve.tensor_tensor(rows, ps_o[s][i][:, :, :], rows, ALU.add)
                ins.then_inc(x1_ready, 1)
                dve.wait_ge(x1_ready, b + 1 + 2)
                for j in range(QT):
                    dve.bn_stats(stats[:, j, :], x1[:, b * QT + j, :]).then_inc(ln_step, 1)
                for j in range(QT):
                    dve.wait_ge(ln_step, b * ROWS_STEPS + j + 1)
                    dve.bn_aggr(mean_var[:, b * QT + j, :], stats[:, j, :]).then_inc(ln_step, 1)

            def norm(b, s, k):
                dve.wait_ge(x2_stored[s], k * 16)
                dve.wait_ge(T_ready, (b + B) * CH + CH)
                for j in range(QT):
                    t = b * QT + j
                    ins = dve.tensor_scalar(x2[s][:, j, :], x1[:, t, :], mean_var[:, t, 0:1], rstd[:, t:t + 1],
                                            ALU.subtract, ALU.mult)
                ins.then_inc(x2_ready, 1)
                dve.wait_ge(x2_ready, b + 1)
                for j in range(QT):
                    dve.wait_ge(squared, b * QT + j + 1)
                    dve.tensor_tensor_reduce(squares[:, :], x2[s][:, j, :], x2[s][:, j, :], 1.0, 0.0, ALU.mult,
                                             ALU.add, square_sum[:, b * QT + j:b * QT + j + 1]).then_inc(squared, 1)

            for b in range(B):
                add_and_measure(b, b % 2, b // 2 + 1)
            inverse_root(dve, mean_var[:, :, 1], LN_EPS, root, rstd[:, :], ln_step, B * ROWS_STEPS, root_ready, 1)
            for b in range(B):
                norm(b, b % 2, b // 2 + 1)
            dve.wait_ge(squared, NT + 1)
            inverse_root(dve, square_sum[:, :], RMS_EPS, root, rms[:, :], ln_step, B * ROWS_STEPS + ROOT_STEPS,
                         root_ready, 2, scale=1.0 / C)
            dve.tensor_scalar(rms_scaled[:, :], rms[:, :], float(C) ** -0.5, None, ALU.mult).then_inc(logits_ready, 1)
            dve.wait_ge(logits_ready, 1)
            dve.wait_ge(products, 4 * B + 4)
            dve.tensor_tensor(logits[:, :, :], ps_l[:, :, :],
                              rms_scaled[:, :].rearrange("p (i o) -> p i o", o=1).to_broadcast([P, NT, E]), ALU.mult)\
               .then_inc(logits_ready, 1)

        @block.tensor
        def _(pe):
            pe.sem_inc(T_ready, 2 * CH)
            pe.sem_inc(products, 4)
            pe.wait_ge(consts, 3)

            def turn(src, n):
                for c in range(CH):
                    pe.wait_ge(T_copied, n * CH + c + 1)
                    for j in range(QT):
                        ins = pe.transpose(ps_T[c][:, j * P:(j + 1) * P], src[:, j, c * P:(c + 1) * P], ident[:, :])
                    ins.then_inc(T_ready, 1)

            def multiply(out, n, s, weights):
                pe.wait_ge(T_copied, (n + 2) * CH)
                for j in range(QT):
                    for c in range(CH):
                        ins = pe.matmul(out(j), turned[s][:, c, j * P:(j + 1) * P], weights[:, c, :],
                                        start=(c == 0), stop=(c == CH - 1))
                    if j % 2:
                        ins.then_inc(products, 1)

            with pe.Fori(0, B // 2) as i:
                for s in range(2):
                    pe.wait_ge(y_copied, i * 2 + s + 1)
                    turn(y_in[s], i * 2 + s)
                pe.wait_ge(loaded, 16 * N_LOADS)
                for s in range(2):
                    pe.wait_ge(x1_ready, i * 2 + s + 1)
                    multiply(lambda j: ps_o[s][j // 2][:, j % 2, :], i * 2 + s, s, wp)
            pe.wait_ge(wr_ready, CH)
            with pe.Fori(0, B // 2) as i:
                for s in range(2):
                    pe.wait_ge(x2_ready, i * 2 + s + 1)
                    turn(x2[s], i * 2 + s + B)
                for s in range(2):
                    multiply(lambda j: ps_l[:, bass.ds((i * 2 + s) * QT + j, 1), :].rearrange("p o e -> p (o e)"),
                             i * 2 + s + B, s, wr_scaled)


LOWEST = -3.0e38
WHOLE = 1.5 * 2.0 ** 23


def build_routing(nc, a, logits, slot_row, slot_weight, tile_expert):
    with ExitStack() as ctx:
        def sb(name, shape, dt=F32):
            return ctx.enter_context(nc.sbuf_tensor(name, shape, dt))

        def sem(name):
            return ctx.enter_context(nc.semaphore(name))

        top = sb("top", [P, NT])
        shifted = sb("shifted", [P, NT, E])
        probs = sb("probs_d", [P, NT, E])
        total = sb("total", [P, NT])
        others = sb("others", [P, NT, E])
        chosen = [sb(f"chosen{k}", [P, NT, E]) for k in range(TOPK)]
        either = sb("either", [P, NT, E])
        either_h = sb("either_h", [P, NT, E], BF16)
        weight_all = sb("weight_all", [P, NT, E])
        work = sb("work", [P, NT, E])
        weight = [sb(f"weight{k}", [P, NT]) for k in range(TOPK)]
        place = sb("place", [P, NT, E])
        place_k = sb("place_k", [P, NT])
        lo = [sb(f"lo{k}", [P, NT]) for k in range(TOPK)]
        hi = [sb(f"hi{k}", [P, NT]) for k in range(TOPK)]
        count = sb("count", [P, E])
        over = sb("over", [P, E, NT])
        tiles = sb("tiles", [P, E])
        before = sb("before", [P, E, E])
        first_tile = sb("first_tile", [P, E])
        end_tile = sb("end_tile", [P, E])
        ended = sb("ended", [P, SLOT_TILES, E])
        expert_f = sb("expert_f", [P, SLOT_TILES])
        per_expert = sb("per_expert", [P, E])
        lo_onehot = [sb(f"lo_onehot{k}", [P, NT, P]) for k in range(TOPK)]
        hi_onehot = sb("hi_onehot", [P, NT, SLOT_TILES])
        hi_values = [sb(f"hi_values{k}", [P, NT, 2, SLOT_TILES]) for k in range(TOPK)]
        row_plus = sb("row_plus", [P, SLOT_TILES])
        empty = sb("empty", [P, SLOT_TILES])
        lower = sb("lower", [P, E, E])
        earlier = sb("earlier", [P, P], BF16)
        ones_h = sb("ones_h", [P, P], BF16)
        tile_128 = sb("tile_128", [P, NT])
        slot_tile = sb("slot_tile", [P, SLOT_TILES])
        order = sb("order", [P, E])
        column = sb("column", [P, P])
        token = sb("token", [P, NT])
        dump = sb("dump", [P, 1])
        ps_place = ctx.enter_context(nc.psum_tensor("ps_place", [P, NT, E], F32))
        ps_count = ctx.enter_context(nc.psum_tensor("ps_count", [P, NT, E], F32))
        ps_slots = ctx.enter_context(nc.psum_tensor("ps_slots", [P, 2, SLOT_TILES], F32))

        loaded, consts, step = sem("loaded_d"), sem("consts_d"), sem("step_d")
        shifted_ready, exp_ready = sem("shifted_ready"), sem("exp_ready")
        either_ready, placed, onehot_ready, slots_ready = sem("either_ready"), sem("placed"), sem("onehot_ready"), sem("slots_ready")
        N_CONSTS = 11

        block = ctx.enter_context(nc.Block())

        @block.sync
        def _(sp):
            sp.dma_start(per_expert[:, :], a["per_expert_scale"].rearrange("(o n) -> o n", o=1).to_broadcast([P, E]))\
              .then_inc(loaded, 16)

        @block.gpsimd
        def _(pool):
            done = [0]

            def const(ins):
                done[0] += 1
                ins.then_inc(consts, 1)
                pool.wait_ge(consts, done[0])

            const(pool.iota(order[:, :], [[-1, E]], base=E, channel_multiplier=0, allow_small_or_imprecise_dtypes=True))
            const(pool.memset(lower[:, :, :], 1.0))
            const(pool.affine_select(out=lower[:, :, :], in_=lower[:, :, :], compare_op=ALU.is_gt, fill=0.0,
                                     base=0, pattern=[[1, E], [-1, E]], channel_multiplier=0))
            const(pool.memset(earlier[:, :], 1.0))
            const(pool.affine_select(out=earlier[:, :], in_=earlier[:, :], compare_op=ALU.is_gt, fill=0.0,
                                     base=0, pattern=[[1, P]], channel_multiplier=-1))
            const(pool.memset(ones_h[:, :], 1.0))
            for t, pattern, base, per_row in ((tile_128, [[P, NT]], 0, 0), (slot_tile, [[1, SLOT_TILES]], 0, 0),
                                              (column, [[1, P]], 0, 0),
                                              (token, [[P, NT]], 1, 1), (dump, [[0, 1]], DUMP + 1, 1)):
                const(pool.iota(t[:, :], pattern, base=base, channel_multiplier=per_row,
                                allow_small_or_imprecise_dtypes=True))
            assert done[0] == N_CONSTS

        @block.scalar
        def _(act):
            act.wait_ge(shifted_ready, 1)
            act.activation(probs[:, :, :], shifted[:, :, :], ACT.Exp).then_inc(exp_ready, 1)

        @block.vector
        def _(dve):
            done = [0]

            def link(ins):
                done[0] += 1
                ins.then_inc(step, 1)
                dve.wait_ge(step, done[0])

            def along(t, n):
                return t[:, :].rearrange("p (i o) -> p i o", o=1).to_broadcast([P, NT, n])

            def per_tile(t, n):
                return t[:, :].rearrange("p (o e) -> p o e", o=1).to_broadcast([P, NT, n])

            full = [P, NT, E]
            link(dve.tensor_reduce(top[:, :], logits[:, :, :], AX.X, ALU.max))
            dve.tensor_tensor(shifted[:, :, :], logits[:, :, :], along(top, E), ALU.subtract).then_inc(shifted_ready, 1)
            dve.wait_ge(consts, 1)
            link(dve.tensor_tensor(work[:, :, :], logits[:, :, :], along(top, E), ALU.is_equal))
            for k in range(TOPK):
                link(dve.tensor_tensor(work[:, :, :], work[:, :, :], per_tile(order, E), ALU.mult))
                link(dve.tensor_reduce(top[:, :], work[:, :, :], AX.X, ALU.max))
                link(dve.tensor_tensor(chosen[k][:, :, :], work[:, :, :], along(top, E), ALU.is_equal))
                if k == 0:
                    link(dve.scalar_tensor_tensor(others[:, :, :], chosen[0][:, :, :], LOWEST, logits[:, :, :],
                                                  ALU.mult, ALU.add))
                    link(dve.tensor_reduce(top[:, :], others[:, :, :], AX.X, ALU.max))
                    link(dve.tensor_tensor(work[:, :, :], others[:, :, :], along(top, E), ALU.is_equal))
            dve.tensor_tensor(either_h[:, :, :], chosen[0][:, :, :], chosen[1][:, :, :], ALU.add).then_inc(either_ready, 1)
            link(dve.tensor_tensor(either[:, :, :], chosen[0][:, :, :], chosen[1][:, :, :], ALU.add))
            dve.wait_ge(loaded, 16)
            dve.wait_ge(exp_ready, 1)
            link(dve.tensor_reduce(total[:, :], probs[:, :, :], AX.X, ALU.add))
            link(dve.reciprocal(total[:, :], total[:, :]))
            link(dve.tensor_tensor(probs[:, :, :], probs[:, :, :], along(total, E), ALU.mult))
            link(dve.tensor_tensor(work[:, :, :], probs[:, :, :], either[:, :, :], ALU.mult))
            link(dve.tensor_reduce(total[:, :], work[:, :, :], AX.X, ALU.add))
            link(dve.tensor_scalar(top[:, :], total[:, :], 0.0, None, ALU.is_le))
            link(dve.tensor_tensor(total[:, :], total[:, :], top[:, :], ALU.add))
            link(dve.reciprocal(total[:, :], total[:, :]))
            link(dve.tensor_tensor(weight_all[:, :, :], probs[:, :, :], along(total, E), ALU.mult))
            link(dve.tensor_tensor(weight_all[:, :, :], weight_all[:, :, :], per_tile(per_expert, E), ALU.mult))
            for k in range(TOPK):
                link(dve.tensor_tensor(work[:, :, :], weight_all[:, :, :], chosen[k][:, :, :], ALU.mult))
                link(dve.tensor_reduce(weight[k][:, :], work[:, :, :], AX.X, ALU.add))
            dve.wait_ge(placed, 1)
            dve.wait_ge(consts, N_CONSTS)
            link(dve.tensor_reduce(count[:, :], ps_count[:, :, :].rearrange("p i e -> p e i"), AX.X, ALU.add))
            link(dve.tensor_tensor(over[:, :, :], count[:, :].rearrange("p (e o) -> p e o", o=1).to_broadcast([P, E, NT]),
                                   tile_128[:, :].rearrange("p (o i) -> p o i", o=1).to_broadcast([P, E, NT]), ALU.is_gt))
            link(dve.tensor_reduce(tiles[:, :], over[:, :, :], AX.X, ALU.add))
            link(dve.tensor_tensor(before[:, :, :], lower[:, :, :],
                                   tiles[:, :].rearrange("p (o f) -> p o f", o=1).to_broadcast([P, E, E]), ALU.mult))
            link(dve.tensor_reduce(first_tile[:, :], before[:, :, :], AX.X, ALU.add))
            link(dve.tensor_tensor(end_tile[:, :], first_tile[:, :], tiles[:, :], ALU.add))
            link(dve.tensor_scalar(first_tile[:, :], first_tile[:, :], float(P), None, ALU.mult))
            link(dve.tensor_tensor(place[:, :, :], ps_place[:, :, :], per_tile(first_tile, E), ALU.add))
            for k in range(TOPK):
                link(dve.tensor_tensor(work[:, :, :], place[:, :, :], chosen[k][:, :, :], ALU.mult))
                link(dve.tensor_reduce(place_k[:, :], work[:, :, :], AX.X, ALU.add))
                link(dve.tensor_scalar(hi[k][:, :], place_k[:, :], 1.0 / P, -0.5 + 0.5 / P, ALU.mult, ALU.add))
                link(dve.tensor_scalar(hi[k][:, :], hi[k][:, :], WHOLE, None, ALU.add))
                link(dve.tensor_scalar(hi[k][:, :], hi[k][:, :], -WHOLE, None, ALU.add))
                link(dve.scalar_tensor_tensor(lo[k][:, :], hi[k][:, :], -float(P), place_k[:, :], ALU.mult, ALU.add))
                dve.tensor_tensor(lo_onehot[k][:, :, :], per_tile(column, P), along(lo[k], P), ALU.is_equal)\
                   .then_inc(onehot_ready, 1)
                link(dve.tensor_tensor(hi_onehot[:, :, :], per_tile(slot_tile, SLOT_TILES), along(hi[k], SLOT_TILES),
                                       ALU.is_equal))
                for v, value in enumerate((token, weight[k])):
                    dve.tensor_tensor(hi_values[k][:, :, v, :], hi_onehot[:, :, :], along(value, SLOT_TILES), ALU.mult)\
                       .then_inc(onehot_ready, 1)
            shape = [P, SLOT_TILES, E]
            link(dve.tensor_tensor(ended[:, :, :],
                                   slot_tile[:, :].rearrange("p (i o) -> p i o", o=1).to_broadcast(shape),
                                   end_tile[:, :].rearrange("p (o e) -> p o e", o=1).to_broadcast(shape), ALU.is_ge))
            link(dve.tensor_reduce(expert_f[:, :], ended[:, :, :], AX.X, ALU.add))
            link(dve.tensor_scalar(tile_expert[:, :], expert_f[:, :], float(E - 1), None, ALU.min))
            dve.wait_ge(slots_ready, 1)
            link(dve.tensor_copy(row_plus[:, :], ps_slots[:, 0, :]))
            link(dve.tensor_copy(slot_weight[:, :], ps_slots[:, 1, :]))
            link(dve.tensor_scalar(empty[:, :], row_plus[:, :], 0.5, dump[:, 0:1], ALU.is_lt, ALU.mult))
            link(dve.tensor_tensor(row_plus[:, :], row_plus[:, :], empty[:, :], ALU.add))
            link(dve.tensor_scalar(slot_row[:, :], row_plus[:, :], -1.0, None, ALU.add))

        @block.tensor
        def _(pe):
            pe.wait_ge(consts, N_CONSTS)
            pe.wait_ge(either_ready, 1)
            pe.matmul(ps_place[:, :, :], earlier[:, :], either_h[:, :, :], start=True, stop=False)
            for i in range(NT - 1):
                n = NT - 1 - i
                pe.matmul(ps_place[:, i + 1:NT, :], ones_h[:, :], either_h[:, i:i + 1, :].to_broadcast([P, n, E]),
                          start=False, stop=(n == 1))
            pe.matmul(ps_count[:, :, :], ones_h[:, :], either_h[:, :, :], start=True, stop=True).then_inc(placed, 1)
            for k in range(TOPK):
                pe.wait_ge(onehot_ready, (k + 1) * 3)
                for i in range(NT):
                    ins = pe.matmul(ps_slots[:, :, :], lo_onehot[k][:, i, :], hi_values[k][:, i, :, :],
                                    start=(k == 0 and i == 0), stop=(k == TOPK - 1 and i == NT - 1))
            ins.then_inc(slots_ready, 1)


def build_experts(nc, x2_rows, out_rows, slot_row, slot_weight, tile_expert, w_gate, w_down,
                  experts_loaded):
    with ExitStack() as ctx:
        def sb(name, shape, dt=F32):
            return ctx.enter_context(nc.sbuf_tensor(name, shape, dt))

        def sem(name):
            return ctx.enter_context(nc.semaphore(name))

        ident = sb("ident_e", [P, P])
        rows_in = sb("rows_in", [P, 2, 1], I32)
        rows_out = sb("rows_out", [P, 2, 1], I32)
        weight_in = sb("weight_in", [P, 2, 1])
        x_in = [sb(f"x_in_e{i}", [P, C]) for i in range(2)]
        xT = [sb(f"xT_e{i}", [P, CH, P]) for i in range(2)]
        gelu = [sb(f"gelu{i}", [P, HID]) for i in range(2)]
        hidden = [sb(f"hidden{i}", [P, HID]) for i in range(2)]
        hiddenT = [sb(f"hiddenT{i}", [P, HC, P]) for i in range(2)]
        y_out = [sb(f"y_out{i}", [P, C]) for i in range(2)]
        ps_gate = [[ctx.enter_context(nc.psum_tensor(f"ps_gate{i}{j}", [P, HID], F32)) for j in range(2)]
                   for i in range(2)]
        ps_xT = ctx.enter_context(nc.psum_tensor("ps_xT_e", [P, CH, P], F32))
        ps_hT = ctx.enter_context(nc.psum_tensor("ps_hT", [P, HC, P], F32))
        ps_y = [ctx.enter_context(nc.psum_tensor(f"ps_y{i}", [P, C], F32)) for i in range(2)]

        consts = sem("consts_e")
        rows_set, rows_back_set = sem("rows_set"), sem("rows_back_set")
        gathered = [sem(f"gathered{i}") for i in range(2)]
        added = sem("added")
        x_turned, x_copied, gates_ready = sem("x_turned"), sem("x_copied"), sem("gates_ready")
        gelu_ready, hidden_ready, h_turned, h_copied = sem("gelu_ready"), sem("hidden_ready"), sem("h_turned"), sem("h_copied")
        down_ready, y_ready = sem("down_ready"), sem("y_ready")

        pool_passed = sem("pool_passed_e")
        block = ctx.enter_context(nc.Block())
        LAST = SLOT_TILES - 1
        assert LAST % 2 == 0

        def each_tile(eng, body):
            body(0, 0, 1)
            body(1, 1, 1)
            with eng.Fori(1, LAST // 2) as i:
                body(i * 2, 0, i + 1)
                body(i * 2 + 1, 1, i + 1)
            body(LAST, 0, LAST // 2 + 1)

        @block.gpsimd
        def _(pool):
            pool.memset(ident[:, :], 0.0).then_inc(consts, 1)
            pool.wait_ge(consts, 1)
            pool.affine_select(out=ident[:, :], in_=ident[:, :], compare_op=ALU.not_equal, fill=1.0,
                               base=0, pattern=[[-1, P]], channel_multiplier=1).then_inc(consts, 1)
            pool.wait_ge(consts, 2)

            def gather(t, s, k):
                reached(pool, x_turned, t - 1)
                reached_apart(pool, gathered[s], k * 16 - 16, pool_passed)
                pool.tensor_copy(rows_in[:, s, :], slot_row[:, bass.ds(t, 1)]).then_inc(rows_set, 1)
                reached_apart(pool, rows_set, t + 1, pool_passed)
                pool.indirect_dma_start(x_in[s][:, :], None, x2_rows, bass.IndirectOffsetOnAxis(rows_in[:, s, :], 0))\
                    .then_inc(gathered[s], 16)

            def add_back(t, s, k):
                reached_apart(pool, added, t * 16, pool_passed)
                pool.tensor_copy(rows_out[:, s, :], slot_row[:, bass.ds(t, 1)]).then_inc(rows_back_set, 1)
                pool.wait_ge(rows_back_set, t + 1)
                reached_apart(pool, y_ready, t + 1, pool_passed)
                pool.indirect_dma_start(out_rows, bass.IndirectOffsetOnAxis(rows_out[:, s, :], 0), y_out[s][:, :], None,
                                        compute_op=ALU.add).then_inc(added, 16)

            gather(0, 0, 1)
            gather(1, 1, 1)
            gather(2, 0, 2)
            gather(3, 1, 2)
            add_back(0, 0, 1)
            with pool.Fori(1, LAST // 2 - 1) as i:
                gather(i * 2 + 2, 0, i + 2)
                add_back(i * 2 - 1, 1, i)
                gather(i * 2 + 3, 1, i + 2)
                add_back(i * 2, 0, i + 1)
            gather(LAST, 0, LAST // 2 + 1)
            for t in range(LAST - 3, LAST + 1):
                add_back(t, t % 2, t // 2 + 1)
            pool.wait_ge(added, SLOT_TILES * 16)

        @block.scalar
        def _(act):
            def tile(t, s, k):
                act.wait_ge(x_turned, t + 1)
                reached(act, gates_ready, (t - 1) * 2)
                act.activation(xT[s][:, :, :], ps_xT[:, :, :], ACT.Copy).then_inc(x_copied, 1)
                act.wait_ge(gates_ready, t * 2 + 1)
                reached(act, hidden_ready, t - 1)
                act.activation(gelu[s][:, :], ps_gate[s][0][:, :], ACT.Gelu_apprx_tanh).then_inc(gelu_ready, 1)

            each_tile(act, tile)

        @block.vector
        def _(dve):
            def tile(t, s, k):
                dve.wait_ge(gelu_ready, t + 1)
                dve.wait_ge(gates_ready, t * 2 + 2)
                reached(dve, h_turned, t - 1)
                dve.tensor_tensor(hidden[s][:, :], ps_gate[s][1][:, :], gelu[s][:, :], ALU.mult)\
                   .then_inc(hidden_ready, 1)
                dve.wait_ge(h_turned, t + 1)
                reached(dve, down_ready, t - 1)
                dve.tensor_copy(hiddenT[s][:, :, :], ps_hT[:, :, :]).then_inc(h_copied, 1)
                dve.wait_ge(down_ready, t + 1)
                reached(dve, added, t * 16 - 16)
                dve.tensor_scalar(y_out[s][:, :], ps_y[s][:, :], slot_weight[:, bass.ds(t, 1)], None, ALU.mult)\
                   .then_inc(y_ready, 1)

            each_tile(dve, tile)

        @block.tensor
        def _(pe):
            def turn_x(t, s, k):
                pe.wait_ge(gathered[s], k * 16)
                reached(pe, x_copied, t)
                for c in range(CH):
                    ins = pe.transpose(ps_xT[:, c, :], x_in[s][:, c * P:(c + 1) * P], ident[:, :])
                ins.then_inc(x_turned, 1)

            def expert(t):
                return pe.value_load(tile_expert[0:1, bass.ds(t, 1)], min_val=0, max_val=E - 1)

            def gate(t, s, j, e):
                if j == 0:
                    pe.wait_ge(x_copied, t + 1)
                    reached(pe, hidden_ready, t - 1)
                for c in range(CH):
                    ins = pe.matmul(ps_gate[s][j][:, :], xT[s][:, c, :],
                                    w_gate[:, bass.ds(e * (CH * 2 * HID) + (c * 2 + j) * HID, HID)],
                                    start=(c == 0), stop=(c == CH - 1))
                ins.then_inc(gates_ready, 1)

            def turn_hidden(t, s, k):
                pe.wait_ge(hidden_ready, t + 1)
                reached(pe, h_copied, t)
                for c in range(HC):
                    ins = pe.transpose(ps_hT[:, c, :], hidden[s][:, c * P:(c + 1) * P], ident[:, :])
                ins.then_inc(h_turned, 1)

            def down(t, s, e):
                pe.wait_ge(h_copied, t + 1)
                reached(pe, y_ready, t - 1)
                for c in range(HC):
                    ins = pe.matmul(ps_y[s][:, :], hiddenT[s][:, c, :],
                                    w_down[:, bass.ds(e * (HC * C) + c * C, C)], start=(c == 0), stop=(c == HC - 1))
                ins.then_inc(down_ready, 1)

            def tile(t, s, k, more=2):
                e_next = expert(t + 1) if more > 0 else None
                e = expert(t)
                if more > 0:
                    gate(t + 1, 1 - s, 0, e_next)
                turn_hidden(t, s, k)
                if more > 1:
                    turn_x(t + 2, s, k + 1)
                if more > 0:
                    gate(t + 1, 1 - s, 1, e_next)
                down(t, s, e)

            pe.wait_ge(consts, 2)
            pe.wait_ge(experts_loaded, 16 * 2 * E)
            turn_x(0, 0, 1)
            e_first = expert(0)
            gate(0, 0, 0, e_first)
            gate(0, 0, 1, e_first)
            turn_x(1, 1, 1)
            tile(0, 0, 1)
            tile(1, 1, 1)
            with pe.Fori(1, LAST // 2 - 1) as i:
                tile(i * 2, 0, i + 1)
                tile(i * 2 + 1, 1, i + 1)
            tile(LAST - 2, 0, LAST // 2)
            tile(LAST - 1, 1, LAST // 2, more=1)
            tile(LAST, 0, LAST // 2 + 1, more=0)


def build_program(nc, a, out_rows):
    scr = {n: nc.dram_tensor(f"scr_{n}", [B, H, D, NSPLIT, TC if n == "kc" else T], BF16).ap()
           for n in ("q", "k", "qc", "kc")}
    scr["v"] = nc.dram_tensor("scr_v", [B, H // GH, P, STEPS, GH * D], F32).ap()
    x2_rows = nc.dram_tensor("x2_rows", [DUMP + P, C], F32).ap()
    with ExitStack() as ctx:
        def sb(name, shape, dt=F32):
            return ctx.enter_context(nc.sbuf_tensor(name, shape, dt))

        y_all = sb("y_all", [P, NG, QT, GH * D])
        w_gate = sb("w_gate", [P, E * CH * 2 * HID])
        w_down = sb("w_down", [P, E * HC * C])
        logits = sb("logits", [P, NT, E])
        slot_row = sb("slot_row", [P, SLOT_TILES], I32)
        slot_weight = sb("slot_weight", [P, SLOT_TILES])
        tile_expert = sb("tile_expert", [P, SLOT_TILES], I32)
        experts_loaded = ctx.enter_context(nc.semaphore("experts_loaded"))

        first_stacks = Stacks(ctx, nc, 0)
        ones_set = ctx.enter_context(nc.semaphore("ones_set"))

        build_projections(nc, a, scr, first_stacks, ones_set)
        build_attention(nc, scr, first_stacks, ones_set, y_all, (a, w_gate, w_down, experts_loaded))
        build_router_inputs(nc, a, y_all, x2_rows, out_rows, logits)
        build_routing(nc, a, logits, slot_row, slot_weight, tile_expert)
        build_experts(nc, x2_rows, out_rows, slot_row, slot_weight, tile_expert, w_gate, w_down,
                      experts_loaded)


def kernel(**inputs):
    import numpy as np
    import concourse.bacc as bacc
    from concourse.bass_utils import run_bass_kernel_spmd

    def columns(v):
        return v.reshape(-1, P).T

    given = {n.replace("L0_xattn_", "").replace("L0_ffn_", ""): np.asarray(v) for n, v in inputs.items()}
    laid = {n: given[n] for n in ("x", "Wq", "Wk", "Wv", "Wcq", "Wck", "Wcv", "Wp", "bv", "bcv", "bp",
                                  "router_w", "per_expert_scale")}
    laid |= {n: columns(given[n]) for n in ("bq", "bk", "bcq", "bck", "router_scale")}
    laid["ctxT"] = given["ctx_512"].transpose(0, 2, 1)
    laid["gating_w"] = given["gating_w"].reshape(E, 2, HID, CH, P).transpose(4, 0, 3, 1, 2).reshape(P, -1)
    laid["linear_w"] = given["linear_w"].reshape(E, HC, P, C).transpose(2, 0, 1, 3).reshape(P, -1)

    nc = bacc.Bacc("TRN2", target_bir_lowering=False, num_devices=1)
    arrays, args = {}, {}
    for name, v in laid.items():
        v = np.ascontiguousarray(v)
        arrays[f"in_{name}"] = v
        args[name] = nc.dram_tensor(f"in_{name}", v.shape, mybir.dt.from_np(v.dtype), kind="ExternalInput").ap()
    out = nc.dram_tensor("out_rows", [DUMP + P, C], F32, kind="ExternalOutput").ap()
    build_program(nc, args, out)
    r = run_bass_kernel_spmd(nc, [arrays], core_ids=[0])
    return r.results[0]["out_rows"][:DUMP].reshape(B, T, C)
```
